# Optimizing a Trainium2 kernel written in Bass

```python
import numpy as np
import jax
import jax.numpy as jnp

def _softmax(x, axis=-1):
    return jax.nn.softmax(x, axis=axis)

def _gelu(x):
    return jax.nn.gelu(x, approximate=True)

def _silu(x):
    return jax.nn.silu(x)

def _sigmoid(x):
    return jax.nn.sigmoid(x)

def _layernorm(x, axis=-1, eps=1e-05):
    m = jnp.mean(x, axis=axis, keepdims=True)
    v = jnp.var(x, axis=axis, keepdims=True)
    return (x - m) / jnp.sqrt(v + eps)

def _scatter_add(tgt, idx, src, axis=0):
    return tgt.at[idx].add(src)

def _segment_sum(src, seg, n):
    return jax.ops.segment_sum(src, seg, n)
kernel_name = 'mk_xattn_ffn_d1_seqx_r8_a6a0ed'

def setup_inputs(seed: int=0):
    np.random.seed(seed)
    _w = jnp.asarray

    def _rec_inputs():
        import jax
        import jax.numpy as jnp
        _rk = jax.random.key(seed)
        x = 0.0002417 + 0.9998 * jax.random.normal(jax.random.fold_in(_rk, 1), (32, 128, 128), jnp.float32)
        _lenS = 128 - jax.random.randint(jax.random.fold_in(_rk, 7), (32,), 0, max(1, 128 // 4) + 1, jnp.int32)
        _lenS2 = 77 - jax.random.randint(jax.random.fold_in(_rk, 8), (32,), 0, max(1, 77 // 4) + 1, jnp.int32)
        _ctx_1024P = jax.random.normal(jax.random.fold_in(_rk, 11), (32, 16, 128), jnp.float32)
        _ctx_1024c = jax.random.dirichlet(jax.random.fold_in(_rk, 511), 0.3 * jnp.ones((16,), jnp.float32), (32, 77))
        _ctx_1024t = jnp.einsum('bsk,bkd->bsd', _ctx_1024c, _ctx_1024P)
        _ctx_1024t = _ctx_1024t * jax.lax.rsqrt(jnp.mean(jnp.square(_ctx_1024t)) + 1e-12) * 0.953939
        ctx_1024 = -0.000125008 + 0.999885 * (_ctx_1024t + 0.3 * jax.random.normal(jax.random.fold_in(_rk, 611), (32, 77, 128), jnp.float32))
        _validS = jnp.arange(128)[None, :] < _lenS[:, None]
        _validS2 = jnp.arange(77)[None, :] < _lenS2[:, None]
        _causal = jnp.tril(jnp.ones((128, 128), dtype=bool))
        mask_BxSxS2_bk1 = jnp.broadcast_to(_validS2[:, None, :], (32, 128, 77))
        return (x, ctx_1024, mask_BxSxS2_bk1)
    x, ctx_1024, mask_BxSxS2_bk1 = _rec_inputs()

    def _L0_xattn_setup():
        import jax, jax.numpy as jnp
        import numpy as np
        NEG_INF = -1000000000.0
        key = jax.random.key(seed)
        kv, kk, kq, km, kw, kb = jax.random.split(key, 6)
        B, Lq, Lk, D = (8, 128, 512, 128)
        v = jax.random.normal(kv, (B, Lk, D), dtype=jnp.float32)
        k = jax.random.normal(kk, (B, Lk, D), dtype=jnp.float32)
        q = jax.random.normal(kq, (B, Lq, D), dtype=jnp.float32)
        mask = jax.random.randint(km, (B, Lq, Lk), 0, 2) > 0
        W_merge = jax.random.normal(kw, (D, D), dtype=jnp.float32) / np.sqrt(D)
        b_merge = jax.random.normal(kb, (D,), dtype=jnp.float32) * 0.02
        return {'v': v, 'k': k, 'q': q, 'mask': mask, 'W_merge': W_merge, 'b_merge': b_merge}
    _L0_xattn_all = _L0_xattn_setup()
    _L0_xattn_in = {k: v for k, v in _L0_xattn_all.items() if k in ('W_merge', 'b_merge')}
    del _L0_xattn_all

    def _L0_ffn_setup():
        import jax, jax.numpy as jnp
        import numpy as np
        B, S, DIM, FFN, E = (4, 256, 128, 512, 8)
        key = jax.random.key(seed)
        k0, k1, k2, k3 = jax.random.split(key, 4)
        scale = 0.02
        return {'hidden_states': jax.random.normal(k0, (B, S, DIM), jnp.float32), 'router_w': jax.random.normal(k1, (DIM, E), jnp.float32) * scale, 'router_b': jnp.zeros((E,), jnp.float32), 'w1': jax.random.normal(k2, (E, DIM, 2 * FFN), jnp.float32) * scale, 'w2': jax.random.normal(k3, (E, FFN, DIM), jnp.float32) * scale}
    _L0_ffn_all = _L0_ffn_setup()
    _L0_ffn_in = {k: v for k, v in _L0_ffn_all.items() if k in ('router_w', 'router_b', 'w1', 'w2')}
    del _L0_ffn_all
    return {'x': x, 'ctx_1024': ctx_1024, 'mask_BxSxS2_bk1': mask_BxSxS2_bk1, 'L0_xattn_W_merge': _L0_xattn_in['W_merge'], 'L0_xattn_b_merge': _L0_xattn_in['b_merge'], 'L0_ffn_router_w': _L0_ffn_in['router_w'], 'L0_ffn_router_b': _L0_ffn_in['router_b'], 'L0_ffn_w1': _L0_ffn_in['w1'], 'L0_ffn_w2': _L0_ffn_in['w2']}

def reference(x, ctx_1024, mask_BxSxS2_bk1, L0_xattn_W_merge, L0_xattn_b_merge, L0_ffn_router_w, L0_ffn_router_b, L0_ffn_w1, L0_ffn_w2):
    import jax
    import jax.numpy as jnp

    def _L0_xattn_ref(v, k, q, mask, W_merge, b_merge):
        import jax, jax.numpy as jnp
        import numpy as np
        NEG_INF = -1000000000.0
        d_k = q.shape[-1]
        scale = 1.0 / jnp.sqrt(jnp.asarray(d_k, dtype=q.dtype))
        scores = jnp.einsum('bqd,bkd->bqk', q, k) * scale
        scores = jnp.where(mask, jnp.asarray(NEG_INF, dtype=scores.dtype), scores)
        att_map = jax.nn.softmax(scores, axis=-1)
        atted = jnp.einsum('bqk,bkd->bqd', att_map, v)
        atted = jnp.swapaxes(atted, -1, -2)
        return jnp.einsum('bdl,ol->bdo', atted, W_merge) + b_merge

    def _L0_ffn_ref(hidden_states, router_w, router_b, w1, w2):
        import jax, jax.numpy as jnp
        import numpy as np
        B, S, DIM, FFN, E = (4, 256, 128, 512, 8)
        b, s, d = hidden_states.shape
        x = hidden_states.reshape(-1, d)
        logits = x @ router_w + router_b
        route = jax.nn.softmax(logits, axis=1)
        max_prob = jnp.max(route, axis=1, keepdims=True)
        max_ind = jnp.argmax(route, axis=1)
        out = jnp.zeros_like(x)
        num_experts = w1.shape[0]
        for e in range(num_experts):
            h = x @ w1[e]
            a, g = jnp.split(h, 2, axis=1)
            y = jax.nn.silu(a) * g @ w2[e]
            out = jnp.where((max_ind == e)[:, None], y, out)
        out = out * max_prob
        return out.reshape(b, s, d)
    x = x + _L0_xattn_ref(ctx_1024, ctx_1024, _layernorm(x, axis=-1), mask_BxSxS2_bk1, L0_xattn_W_merge, L0_xattn_b_merge)
    x = x + _L0_ffn_ref(_layernorm(x, axis=-1), L0_ffn_router_w, L0_ffn_router_b, L0_ffn_w1, L0_ffn_w2)
    return x

_drawn_inputs = setup_inputs


def setup_inputs(seed=0):
    import zlib

    import numpy as np

    out = dict(_drawn_inputs(seed))
    spreads = {'L0_ffn_router_b': (0.0, 0.8)}
    factors = {'L0_xattn_b_merge': 2.845, 'L0_ffn_router_w': 8.0, 'L0_ffn_w1': 8.0, 'L0_ffn_w2': 8.0}
    for name, (base, spread) in spreads.items():
        noise = np.random.default_rng([zlib.crc32(name.encode()), seed]).standard_normal(out[name].shape)
        drawn = base * np.exp(spread * noise) if base else spread * noise
        out[name] = jnp.asarray(drawn.astype(out[name].dtype))
    for name, factor in factors.items():
        out[name] = (out[name] * factor).astype(out[name].dtype)
    return out
```

```python
from contextlib import ExitStack

import numpy as np
import concourse.bass as bass
from concourse import mybir

ALU = mybir.AluOpType
ACT = mybir.ActivationFunctionType
AX = mybir.AxisListType
F32 = mybir.dt.float32
F32R = mybir.dt.float32r
BF16 = mybir.dt.bfloat16
I32 = mybir.dt.int32
U32 = mybir.dt.uint32

P = 128
B, S, D = 32, 128, 128
K = 77
E, F = 8, 512
TOKENS = B * S
GB = 4
NG = B // GB
TILES = TOKENS // P + E - 1
TPAD = TILES + TILES % 2
ROW = D + 4
MEAN, RSTD, PROB = D, D + 1, D + 2
FC = F // P
WCH = 512
NW1 = E * 2 * F // WCH
NW2 = E * F * D // P // WCH
NWP = NW1 + NW2
BPOOL, BSTEP = 8, 8
WRING = 6
SCALE = float(1.0 / np.sqrt(np.float32(D)))
NEG = -1.0e9
EPS = 1.0e-5
ROUND = 1.5 * 2.0 ** 23
FAR = 2 * TOKENS

C_ID, C_CEN, C_TRI, C_IOTA = 0, P, 2 * P, 3 * P
C_TOK = 4 * P
C_KEEP = C_TOK + B
C_EM = C_KEEP + B * E
C_ONE = C_EM + E
C_ALL = C_ONE + E


def constants():
    c = np.zeros((P, C_ALL), np.float32)
    c[:, C_ID:C_ID + P] = np.eye(P)
    c[:, C_CEN:C_CEN + P] = np.eye(P) - 1.0 / P
    c[:, C_TRI:C_TRI + P] = np.triu(np.ones((P, P)), 1)
    c[:, C_IOTA:C_IOTA + P] = np.arange(P)
    c[:, C_TOK:C_TOK + B] = np.arange(P)[:, None] * B + np.arange(B)[None] + 1
    c[:, C_KEEP:C_KEEP + B * E] = np.tile(np.arange(B) > 0, E)
    c[:, C_EM:C_EM + E] = np.arange(E) - E
    c[:, C_ONE:C_ONE + E] = 1.0
    return c


def build(nc, x, ctx_k, ctx_t, ctx_one, mask, w_t, b_merge, router_w, router_b, w1, w2, const, out):
    x1_rows = nc.dram_tensor("x1_rows", (TOKENS, ROW), F32, kind="Internal").ap()

    with ExitStack() as keep:
        def sb(name, shape, dt=F32, stack=keep):
            return stack.enter_context(nc.sbuf_tensor(name, shape, dt))

        def sem(name):
            return keep.enter_context(nc.semaphore(name))

        cst = sb("cst", [P, C_ALL])
        w1hi = sb("w1hi", [P, E * 2 * F], F32R)
        w1lo = sb("w1lo", [P, E * 2 * F], F32R)
        w2hi = sb("w2hi", [P, E * FC * D], F32R)
        w2lo = sb("w2lo", [P, E * FC * D], F32R)
        x1 = sb("x1", [P, B, ROW])
        onehot = sb("onehot", [P, E, B], BF16)
        tri = sb("tri", [P, P], BF16)
        ones = sb("ones", [P, P], BF16)
        gather_at = sb("gather_at", [P, TPAD], U32)
        scatter_at = sb("scatter_at", [P, TPAD], U32)
        tile_expert = sb("tile_expert", [P, TPAD], I32)

        early = ExitStack()
        xs = sb("xs", [P, B, D], F32, early)
        ctxk = sb("ctxk", [K + 1, 2, GB * D], F32, early)
        ctxt = sb("ctxt", [P, 2, GB * K], F32, early)
        ctxc = sb("ctxc", [P, 2, GB * K], F32, early)
        msk = sb("msk", [P, B * K], mybir.dt.uint8, early)
        wt = sb("wt", [P, D], F32, early)
        rw = sb("rw", [P, E], F32, early)
        rwc = sb("rwc", [P, E], F32, early)
        rb = sb("rb", [P, E], F32, early)
        xt = sb("xt", [P, 2, GB * S], F32, early)
        prob = sb("prob", [P, 2, GB, K], F32, early)
        att = sb("att", [P, 2, GB, K], F32, early)
        merged = sb("merged", [K + 1, 2, GB * D], F32, early)
        x1t = sb("x1t", [P, 2, GB * S], F32, early)
        wraw = sb("wraw", [P, WRING, WCH], F32, early)
        bn = sb("bn", [P, 2, GB, 6], F32, early)
        mv = sb("mv", [P, B, 2], F32, early)
        half = sb("half", [P, GB], F32, early)
        ve = sb("ve", [P, B], F32, early)
        rstd = sb("rstd", [P, B], F32, early)
        rs = sb("rs", [P, B], F32, early)
        fill = sb("fill", [P, B], F32, early)
        nmax = sb("nmax", [P, B], F32, early)
        nbias = sb("nbias", [P, B], F32, early)
        esum = sb("esum", [P, B], F32, early)
        einv = sb("einv", [P, B], F32, early)
        ve2 = sb("ve2", [P, B], F32, early)
        lg0 = sb("lg0", [P, B, E], F32, early)
        lg = sb("lg", [P, B, E], F32, early)
        lmax = sb("lmax", [P, B], F32, early)
        ldif = sb("ldif", [P, B, E], F32, early)
        lexp = sb("lexp", [P, B, E], F32, early)
        lsum = sb("lsum", [P, B], F32, early)
        cand = sb("cand", [P, B, E], F32, early)
        emin = sb("emin", [P, B], F32, early)
        early.close()

        late = keep
        pre = sb("pre", [P, E, B])
        tl0 = sb("tl0", [P, E])
        tl = sb("tl", [P, E])
        tend = sb("tend", [P, E])
        tbeg = sb("tbeg", [P, E])
        sl0 = sb("sl0", [P, E, B])
        sl1 = sb("sl1", [P, E, B])
        sl2 = sb("sl2", [P, E, B])
        sl3 = sb("sl3", [P, E, B])
        slot = sb("slot", [P, B])
        jt0 = sb("jt0", [P, B])
        jt = sb("jt", [P, B])
        rm = sb("rm", [P, B])
        tcmp = sb("tcmp", [P, TPAD, E])
        tcnt = sb("tcnt", [P, TPAD])
        vz = sb("vz", [P, TPAD])
        a0 = sb("a0", [P, B, TPAD])
        amat = sb("amat", [P, B, TPAD], F32R)
        bmat = sb("bmat", [P, B, P], F32R)
        rows = sb("rows", [P, TILES, ROW])
        hg = sb("hg", [P, 2, D])
        hthi = sb("hthi", [P, 2, P], F32R)
        htlo = sb("htlo", [P, 2, P], F32R)
        sa = sb("sa", [P, 2, F])
        u = sb("u", [P, 2, F])
        uthi = sb("uthi", [P, 2, F], F32R)
        utlo = sb("utlo", [P, 2, F], F32R)

        bank = [keep.enter_context(nc.psum_tensor(f"bank{i}", [P, 512], F32)) for i in range(8)]
        ps_xt, ps_cc, ps_s, ps_g, ps_o, ps_x1t, ps_l = bank[0], bank[1], bank[2:4], bank[4], bank[5], bank[6], bank[7]
        ps_rank, ps_cnt, ps_inv = bank[0], bank[1], bank[2]
        ps_a, ps_g3, ps_ut, ps_ht, ps_y = bank[0:2], bank[2:4], bank[4:6], bank[6], bank[7]

        l_const, l_small, l_mask, l_ones = sem("l_const"), sem("l_small"), sem("l_mask"), sem("l_ones")
        l_x = [sem(f"l_x{g}") for g in range(NG)]
        l_ctxk = [sem(f"l_ctxk{i}") for i in range(2)]
        l_ctxt = [sem(f"l_ctxt{i}") for i in range(2)]
        l_w = [sem(f"l_w{i}") for i in range(WRING)]
        s_rows = sem("s_rows")
        p_xt, p_cc, p_s, p_g, p_o, p_x1t, p_l = (sem(n) for n in ("p_xt", "p_cc", "p_s", "p_g", "p_o", "p_x1t", "p_l"))
        p_rwc = sem("p_rwc")
        a_xt, a_cc, a_exp, a_g, a_x1t, a_rexp, a_whi = (sem(n) for n in ("a_xt", "a_cc", "a_exp", "a_g", "a_x1t", "a_rexp", "a_whi"))
        v_bf, v_rwc, v_bn, v_mv, v_rs, v_fill, v_mask, v_max, v_nb, v_inv, v_att = (
            sem(n) for n in ("v_bf", "v_rwc", "v_bn", "v_mv", "v_rs", "v_fill", "v_mask", "v_max", "v_nb", "v_inv", "v_att"))
        v_x1, v_bn2, v_mv2, v_lg0, v_lg, v_lmax, v_ldif, v_cand, v_emin, v_hot, v_lsum, v_prob = (
            sem(n) for n in ("v_x1", "v_bn2", "v_mv2", "v_lg0", "v_lg", "v_lmax", "v_ldif", "v_cand", "v_emin", "v_hot", "v_lsum", "v_prob"))
        g_half, g_ve, g_rstd, g_ve2, g_rstd2, g_wlo = (sem(n) for n in ("g_half", "g_ve", "g_rstd", "g_ve2", "g_rstd2", "g_wlo"))
        p_rank, p_inv = sem("p_rank"), sem("p_inv")
        v_chain = sem("v_chain")
        v_rm, v_bm, g_bm, v_am, v_gat, v_sca, v_te = (sem(n) for n in ("v_rm", "v_bm", "g_bm", "v_am", "v_gat", "v_sca", "v_te"))
        g_rows = [sem(f"g_rows{i}") for i in range(2)]
        g_out = sem("g_out")
        p_ht, p_a, p_gg, p_ut, p_y = (sem(n) for n in ("p_ht", "p_a", "p_gg", "p_ut", "p_y"))
        a_hthi, a_sa, a_uthi = sem("a_hthi"), sem("a_sa"), sem("a_uthi")
        v_hg, v_htlo, v_u, v_utlo, v_y = sem("v_hg"), sem("v_htlo"), sem("v_u"), sem("v_utlo"), sem("v_y")

        def group(t, g):
            return t[:, GB * g:GB * g + GB]

        def wpiece(i):
            hi, lo, j = (w1hi, w1lo, i) if i < NW1 else (w2hi, w2lo, i - NW1)
            return hi[:, j * WCH:(j + 1) * WCH], lo[:, j * WCH:(j + 1) * WCH]

        def k_of(k, off):
            return k + off if isinstance(k, int) else TILES // 2

        def run_steps(eng, step, begin):
            for k in range(begin, 2):
                step(k, odd=k % 2)
            with eng.Fori(2, TILES - 3, 2) as k:
                step(k, odd=0)
                step(k + 1, odd=1)
            for k in range(TILES - 3, TILES + 2):
                step(k, odd=k % 2)

        block = keep.enter_context(nc.Block())

        @block.sync
        def _(sp):
            sp.dma_start(cst[:], const).then_inc(l_const, 16)

            def load_w(i):
                if i >= WRING:
                    sp.wait_ge(a_whi, i - WRING + 1)
                    sp.wait_ge(g_wlo, i - WRING + 1)
                src = w1[:, i * WCH:(i + 1) * WCH] if i < NW1 else w2[:, (i - NW1) * WCH:(i - NW1 + 1) * WCH]
                sp.dma_start(wraw[:, i % WRING, :], src).then_inc(l_w[i % WRING], 16)

            def store_rows(g):
                sp.wait_ge(v_prob, g + 1)
                sp.wait_ge(g_rstd2, g + 1)
                sp.dma_start(x1_rows.rearrange("(l b) c -> l b c", b=B)[:, GB * g:GB * g + GB, :],
                             group(x1, g)).then_inc(s_rows, 16)

            for g in range(NG):
                sp.dma_start(group(xs, g), x[:, GB * g:GB * g + GB, :]).then_inc(l_x[g], 16)
                if g >= 2:
                    sp.wait_ge(p_cc, g - 1)
                sp.dma_start(ctxt[:, g % 2, :], ctx_t[:, g * GB * K:(g + 1) * GB * K]).then_inc(l_ctxt[g % 2], 16)
                if g == 0:
                    sp.dma_start(msk[:], mask).then_inc(l_mask, 16)
                    sp.dma_start(wt[:], w_t).then_inc(l_small, 16)
                    sp.dma_start(rw[:], router_w).then_inc(l_small, 16)
                    sp.dma_start(rb[:], router_b.partition_broadcast(P)).then_inc(l_small, 16)
                    for i in range(2):
                        sp.dma_start(ctxk[K:K + 1, i, :], ctx_one).then_inc(l_ones, 16)
                        for j in range(GB):
                            sp.dma_start(merged[K:K + 1, i, j * D:(j + 1) * D], b_merge).then_inc(l_ones, 16)
                if g >= 2:
                    sp.wait_ge(p_o, g - 1)
                sp.dma_start(ctxk[0:K, g % 2, :], ctx_k[:, g * GB * D:(g + 1) * GB * D]).then_inc(l_ctxk[g % 2], 16)
                for i in range(NWP * g // NG, NWP * (g + 1) // NG):
                    load_w(i)
                if g >= 4:
                    store_rows(g - 4)
            for g in range(NG - 4, NG):
                store_rows(g)

        @block.gpsimd
        def _(pool):
            nc.gpsimd.memset(half[:], -0.5).then_inc(g_half, 1)
            pool.wait_ge(g_half, 1)

            def w_lo(i):
                hi, lo = wpiece(i)
                pool.wait_ge(a_whi, i + 1)
                pool.tensor_tensor(lo, wraw[:, i % WRING, :], hi.bitcast(F32), ALU.subtract).then_inc(g_wlo, 1)

            def rstd1(g):
                pool.wait_ge(v_mv, g + 1)
                pool.tensor_scalar(group(ve, g), mv[:, GB * g:GB * g + GB, 1], EPS, None, ALU.add).then_inc(g_ve, 1)
                pool.wait_ge(g_ve, g + 1)
                pool.tensor_tensor(group(rstd, g), group(ve, g), half[:], ALU.pow).then_inc(g_rstd, 1)

            def rstd2(g):
                pool.wait_ge(v_mv2, g + 1)
                pool.tensor_scalar(group(ve2, g), x1[:, GB * g:GB * g + GB, RSTD], EPS, None, ALU.add).then_inc(g_ve2, 1)
                pool.wait_ge(g_ve2, g + 1)
                pool.tensor_tensor(x1[:, GB * g:GB * g + GB, RSTD], group(ve2, g), half[:], ALU.pow).then_inc(g_rstd2, 1)

            rstd1(0)
            done = 0
            for k in range(NG + 2):
                if 1 <= k + 1 < NG:
                    rstd1(k + 1)
                if 0 <= k - 2 < NG:
                    rstd2(k - 2)
                while done < min(NWP, NWP * (k + 1) // NG):
                    w_lo(done)
                    done += 1

            pool.wait_ge(v_rm, 1)
            for b in range(B - BPOOL, B):
                pool.tensor_scalar(bmat[:, b, :], cst[:, C_IOTA:C_IOTA + P], rm[:, b:b + 1], None, ALU.is_equal).then_inc(g_bm, 1)

            def gather(i):
                if i == 0:
                    pool.wait_ge(v_gat, 1)
                    pool.wait_ge(s_rows, 16 * NG)
                if i >= 2:
                    pool.wait_ge(g_rows[i % 2], 16 * (i // 2))
                pool.indirect_dma_start(rows[:, i, :], None, x1_rows,
                                        bass.IndirectOffsetOnAxis(gather_at[:, i:i + 1], 0)).then_inc(g_rows[i % 2], 16)

            def scatter(i):
                if i == 0:
                    pool.wait_ge(v_sca, 1)
                pool.wait_ge(v_y, i + 1)
                pool.indirect_dma_start(out, bass.IndirectOffsetOnAxis(scatter_at[:, i:i + 1], 0), rows[:, i, 0:D], None,
                                        bounds_check=TOKENS - 1, oob_is_err=False).then_inc(g_out, 16)

            for i in range(TILES + 5):
                if i < TILES:
                    gather(i)
                if i >= 5:
                    scatter(i - 5)
            pool.wait_ge(g_out, 16 * TILES)

        @block.scalar
        def _(act):
            def w_hi(i):
                hi, _ = wpiece(i)
                act.wait_ge(l_w[i % WRING], 16 * (i // WRING + 1))
                act.activation(hi, wraw[:, i % WRING, :], ACT.Copy).then_inc(a_whi, 1)

            done = 0
            for k in range(NG + 4):
                g = k - 2
                if 0 <= g < NG:
                    act.wait_ge(p_g, g + 1)
                    if g >= 2:
                        act.wait_ge(p_o, g - 1)
                    act.activation(merged[0:K, g % 2, :], ps_g[0:K, :], ACT.Copy).then_inc(a_g, 1)
                g = k
                if g < NG:
                    act.wait_ge(p_xt, g + 1)
                    if g >= 2:
                        act.wait_ge(p_s, g - 1)
                    act.activation(xt[:, g % 2, :], ps_xt[:, :], ACT.Copy).then_inc(a_xt, 1)
                    act.wait_ge(p_cc, g + 1)
                    act.activation(ctxc[:, g % 2, :], ps_cc[:, 0:GB * K], ACT.Copy).then_inc(a_cc, 1)
                g = k - 1
                if 0 <= g < NG:
                    act.wait_ge(v_nb, g + 1)
                    act.wait_ge(v_rs, g + 1)
                    if g >= 2:
                        act.wait_ge(v_att, g - 1)
                    for j in range(GB):
                        b = GB * g + j
                        act.activation(prob[:, g % 2, j, :], ps_s[g % 2][:, j * K:(j + 1) * K], ACT.Exp,
                                       bias=nbias[:, b:b + 1], scale=rs[:, b:b + 1],
                                       accum_out=esum[:, b:b + 1]).then_inc(a_exp, 1)
                g = k - 3
                if 0 <= g < NG:
                    act.wait_ge(p_x1t, g + 1)
                    if g >= 2:
                        act.wait_ge(p_l, g - 1)
                    act.activation(x1t[:, g % 2, :], ps_x1t[:, :], ACT.Copy).then_inc(a_x1t, 1)
                    act.wait_ge(v_ldif, g + 1)
                    act.activation(group(lexp, g), group(ldif, g), ACT.Exp).then_inc(a_rexp, 1)
                while done < min(NWP, NWP * (k + 1) // NG):
                    w_hi(done)
                    done += 1

            def step(k, odd=0):
                if 0 <= k_of(k, 1) < TILES:
                    q = (odd + 1) % 2
                    act.wait_ge(p_ht, k + 2)
                    if k_of(k, 1) >= 2:
                        act.wait_ge(p_gg, k)
                    act.activation(hthi[:, q, :], ps_ht[:, 0:P], ACT.Copy).then_inc(a_hthi, 1)
                if 0 <= k_of(k, 0) < TILES:
                    act.wait_ge(p_a, k + 1)
                    if k_of(k, 0) >= 2:
                        act.wait_ge(v_u, k - 1)
                    act.activation(sa[:, odd, :], ps_a[odd][:, :], ACT.Silu).then_inc(a_sa, 1)
                if 0 <= k_of(k, -1) < TILES:
                    q = (odd + 1) % 2
                    act.wait_ge(p_ut, k)
                    if k_of(k, -1) >= 2:
                        act.wait_ge(p_y, k - 2)
                    act.activation(uthi[:, q, :], ps_ut[q][:, :], ACT.Copy).then_inc(a_uthi, 1)

            run_steps(act, step, -1)

        @block.vector
        def _(dve):
            dve.wait_ge(l_const, 16)
            dve.tensor_copy(tri[:], cst[:, C_TRI:C_TRI + P]).then_inc(v_bf, 1)
            dve.memset(ones[:], 1.0).then_inc(v_bf, 1)
            dve.wait_ge(p_rwc, 1)
            dve.tensor_copy(rwc[:], ps_l[:, 0:E]).then_inc(v_rwc, 1)

            def stats1(g):
                dve.wait_ge(l_x[g], 16)
                if g >= 1:
                    dve.wait_ge(v_mv, g)
                for j in range(GB):
                    dve.bn_stats(bn[:, 0, j, :], xs[:, GB * g + j, :]).then_inc(v_bn, 1)
                dve.wait_ge(v_bn, GB * (g + 1))
                for j in range(GB):
                    last = dve.bn_aggr(mv[:, GB * g + j, :], bn[:, 0, j, :])
                last.then_inc(v_mv, 1)

            def scales(g):
                dve.wait_ge(g_rstd, g + 1)
                dve.tensor_scalar(group(rs, g), group(rstd, g), SCALE, None, ALU.mult).then_inc(v_rs, 1)
                dve.scalar_tensor_tensor(group(fill, g), group(ve, g), NEG / SCALE, group(rstd, g), ALU.mult, ALU.mult).then_inc(v_fill, 1)

            def softmax_head(g):
                s3 = ps_s[g % 2][:, 0:GB * K].rearrange("p (b k) -> p b k", b=GB)
                dve.wait_ge(p_s, g + 1)
                dve.wait_ge(v_fill, g + 1)
                if g == 0:
                    dve.wait_ge(l_mask, 16)
                dve.copy_predicated(s3, msk[:, g * GB * K:(g + 1) * GB * K].rearrange("p (b k) -> p b k", b=GB),
                                    group(fill, g).unsqueeze(2).to_broadcast([P, GB, K])).then_inc(v_mask, 1)
                dve.wait_ge(v_mask, g + 1)
                dve.tensor_reduce(group(nmax, g), s3, AX.X, ALU.max, negate=True).then_inc(v_max, 1)
                dve.wait_ge(v_max, g + 1)
                dve.wait_ge(v_rs, g + 1)
                dve.tensor_tensor(group(nbias, g), group(nmax, g), group(rs, g), ALU.mult).then_inc(v_nb, 1)

            def softmax_tail(g):
                dve.wait_ge(a_exp, GB * (g + 1))
                dve.reciprocal(group(einv, g), group(esum, g)).then_inc(v_inv, 1)
                dve.wait_ge(v_inv, g + 1)
                if g >= 2:
                    dve.wait_ge(p_g, g - 1)
                dve.tensor_tensor(att[:, g % 2], prob[:, g % 2], group(einv, g).unsqueeze(2).to_broadcast([P, GB, K]),
                                  ALU.mult).then_inc(v_att, 1)

            def residual(g):
                dve.wait_ge(p_o, g + 1)
                dve.wait_ge(l_x[g], 16)
                dve.tensor_tensor(x1[:, GB * g:GB * g + GB, 0:D], ps_o[:, :].rearrange("p (b d) -> p b d", b=GB),
                                  group(xs, g), ALU.add).then_inc(v_x1, 1)
                dve.wait_ge(v_x1, g + 1)
                if g >= 1:
                    dve.wait_ge(v_mv2, g)
                for j in range(GB):
                    dve.bn_stats(bn[:, 1, j, :], x1[:, GB * g + j, 0:D]).then_inc(v_bn2, 1)
                dve.wait_ge(v_bn2, GB * (g + 1))
                for j in range(GB):
                    last = dve.bn_aggr(x1[:, GB * g + j, MEAN:RSTD + 1], bn[:, 1, j, :])
                last.then_inc(v_mv2, 1)

            def router(g):
                gb = slice(GB * g, GB * g + GB)
                wide = [P, GB, E]
                dve.wait_ge(p_l, g + 1)
                dve.wait_ge(g_rstd2, g + 1)
                dve.tensor_tensor(lg0[:, gb, :], ps_l[:, 0:GB * E].rearrange("p (b e) -> p b e", b=GB),
                                  x1[:, gb, RSTD].unsqueeze(2).to_broadcast(wide), ALU.mult).then_inc(v_lg0, 1)
                dve.wait_ge(v_lg0, g + 1)
                dve.tensor_tensor(lg[:, gb, :], lg0[:, gb, :], rb[:].unsqueeze(1).to_broadcast(wide), ALU.add).then_inc(v_lg, 1)
                dve.wait_ge(v_lg, g + 1)
                dve.tensor_reduce(lmax[:, gb], lg[:, gb, :], AX.X, ALU.max).then_inc(v_lmax, 1)
                dve.wait_ge(v_lmax, g + 1)
                dve.tensor_tensor(ldif[:, gb, :], lg[:, gb, :], lmax[:, gb].unsqueeze(2).to_broadcast(wide), ALU.subtract).then_inc(v_ldif, 1)
                dve.wait_ge(v_ldif, g + 1)
                dve.scalar_tensor_tensor(cand[:, gb, :], ldif[:, gb, :], 0.0,
                                         cst[:, C_EM:C_EM + E].unsqueeze(1).to_broadcast(wide), ALU.is_ge, ALU.mult).then_inc(v_cand, 1)
                dve.wait_ge(v_cand, g + 1)
                dve.tensor_reduce(emin[:, gb], cand[:, gb, :], AX.X, ALU.min).then_inc(v_emin, 1)
                dve.wait_ge(v_emin, g + 1)
                dve.tensor_tensor(onehot[:, :, gb].rearrange("p e b -> p b e"), cst[:, C_EM:C_EM + E].unsqueeze(1).to_broadcast(wide),
                                  emin[:, gb].unsqueeze(2).to_broadcast(wide), ALU.is_equal).then_inc(v_hot, 1)
                dve.wait_ge(a_rexp, g + 1)
                dve.tensor_reduce(lsum[:, gb], lexp[:, gb, :], AX.X, ALU.add).then_inc(v_lsum, 1)
                dve.wait_ge(v_lsum, g + 1)
                dve.reciprocal(x1[:, gb, PROB], lsum[:, gb]).then_inc(v_prob, 1)

            dve.memset(x1[:, :, PROB + 1:ROW], 0.0).then_inc(v_bf, 1)
            dve.wait_ge(l_small, 48)
            stats1(0)
            for k in range(NG + 4):
                if k < NG:
                    scales(k)
                if 0 <= k - 1 < NG:
                    softmax_head(k - 1)
                if k + 1 < NG:
                    stats1(k + 1)
                if 0 <= k - 1 < NG:
                    softmax_tail(k - 1)
                if 0 <= k - 2 < NG:
                    residual(k - 2)
                if 0 <= k - 3 < NG:
                    router(k - 3)

            steps = [0]

            def then(ins):
                steps[0] += 1
                ins.then_inc(v_chain, 1)
                dve.wait_ge(v_chain, steps[0])

            dve.wait_ge(p_rank, 1)
            cnt3 = ps_cnt[:, 0:E * B].rearrange("p (e b) -> p e b", e=E)
            rank3 = ps_rank[:, 0:E * B].rearrange("p (e b) -> p e b", e=E)
            wide = [P, E, B]
            then(dve.tensor_tensor_scan(pre[:].rearrange("p e b -> p (e b)"), cst[:, C_KEEP:C_KEEP + E * B],
                                        ps_cnt[:, 0:E * B], 0.0, ALU.mult, ALU.add))
            then(dve.tensor_scalar(tl0[:], pre[:, :, B - 1], P / 2 - 0.5, 1.0 / P, ALU.add, ALU.mult))
            then(dve.tensor_scalar(tl[:], tl0[:], ROUND, ROUND, ALU.add, ALU.subtract))
            then(dve.tensor_tensor_scan(tend[:], cst[:, C_ONE:C_ONE + E], tl[:], 0.0, ALU.mult, ALU.add))
            then(dve.tensor_tensor(tbeg[:], tend[:], tl[:], ALU.subtract))
            then(dve.tensor_tensor(sl0[:], pre[:], cnt3, ALU.subtract))
            then(dve.tensor_tensor(sl1[:], sl0[:], rank3, ALU.add))
            then(dve.scalar_tensor_tensor(sl2[:], tbeg[:].unsqueeze(2).to_broadcast(wide), float(P), sl1[:], ALU.mult, ALU.add))
            then(dve.tensor_tensor(sl3[:], sl2[:], onehot[:], ALU.mult))
            then(dve.tensor_reduce(slot[:], sl3[:].rearrange("p e b -> p b e"), AX.X, ALU.add))
            then(dve.tensor_scalar(jt0[:], slot[:], -(P / 2 - 0.5), 1.0 / P, ALU.add, ALU.mult))
            then(dve.tensor_scalar(jt[:], jt0[:], ROUND, ROUND, ALU.add, ALU.subtract))
            dve.scalar_tensor_tensor(rm[:], jt[:], -float(P), slot[:], ALU.mult, ALU.add).then_inc(v_rm, 1)
            wide = [P, B, TPAD]
            then(dve.tensor_tensor(a0[:], cst[:, C_IOTA:C_IOTA + TPAD].unsqueeze(1).to_broadcast(wide),
                                   jt[:].unsqueeze(2).to_broadcast(wide), ALU.is_equal))
            dve.tensor_tensor(amat[:], a0[:], cst[:, C_TOK:C_TOK + B].unsqueeze(2).to_broadcast(wide), ALU.mult).then_inc(v_am, 1)
            dve.wait_ge(v_rm, 1)
            for b in range(0, B - BPOOL, BSTEP):
                wide = [P, BSTEP, P]
                dve.tensor_tensor(bmat[:, b:b + BSTEP, :], cst[:, C_IOTA:C_IOTA + P].unsqueeze(1).to_broadcast(wide),
                                  rm[:, b:b + BSTEP].unsqueeze(2).to_broadcast(wide), ALU.is_equal).then_inc(v_bm, 1)
            wide = [P, TPAD, E]
            then(dve.tensor_tensor(tcmp[:], tend[:].unsqueeze(1).to_broadcast(wide),
                                   cst[:, C_IOTA:C_IOTA + TPAD].unsqueeze(2).to_broadcast(wide), ALU.is_le))
            then(dve.tensor_reduce(tcnt[:], tcmp[:], AX.X, ALU.add))
            dve.tensor_scalar(tile_expert[:], tcnt[:], float(E - 1), None, ALU.min).then_inc(v_te, 1)
            dve.wait_ge(p_inv, 1)
            inv = ps_inv[:, 0:TPAD]
            dve.tensor_scalar(gather_at[:], inv, 1.0, 1.0, ALU.max, ALU.subtract).then_inc(v_gat, 1)
            then(dve.tensor_scalar(vz[:], inv, 0.0, float(FAR + 1), ALU.is_equal, ALU.mult))
            dve.scalar_tensor_tensor(scatter_at[:], inv, -1.0, vz[:], ALU.add, ALU.add).then_inc(v_sca, 1)

            def step(k, odd=0):
                q = (odd + 1) % 2
                if 0 <= k_of(k, 2) < TILES:
                    if isinstance(k, int):
                        dve.wait_ge(g_rows[odd], 16 * ((k + 2) // 2 + 1))
                    else:
                        dve.wait_ge(g_rows[odd], (k - odd) * 8 + 32)
                    if k_of(k, 2) >= 2:
                        dve.wait_ge(p_ht, k + 1)
                    row = rows[:, bass.ds(k + 2, 1), :].squeeze(1) if not isinstance(k, int) else rows[:, k + 2, :]
                    dve.tensor_scalar(hg[:, odd, :], row[:, 0:D], row[:, MEAN:MEAN + 1], row[:, RSTD:RSTD + 1],
                                      ALU.subtract, ALU.mult).then_inc(v_hg, 1)
                if 0 <= k_of(k, 1) < TILES:
                    dve.wait_ge(a_hthi, k + 2)
                    if k_of(k, 1) >= 2:
                        dve.wait_ge(p_gg, k)
                    dve.tensor_tensor(htlo[:, q, :], ps_ht[:, 0:P], hthi[:, q, :].bitcast(F32), ALU.subtract).then_inc(v_htlo, 1)
                if 0 <= k_of(k, 0) < TILES:
                    dve.wait_ge(p_gg, k + 1)
                    dve.wait_ge(a_sa, k + 1)
                    if k_of(k, 0) >= 2:
                        dve.wait_ge(p_ut, k - 1)
                    dve.tensor_tensor(u[:, odd, :], ps_g3[odd][:, :], sa[:, odd, :], ALU.mult).then_inc(v_u, 1)
                if 0 <= k_of(k, -1) < TILES:
                    dve.wait_ge(a_uthi, k)
                    if k_of(k, -1) >= 2:
                        dve.wait_ge(p_y, k - 2)
                    dve.tensor_tensor(utlo[:, q, :], ps_ut[q][:, :], uthi[:, q, :].bitcast(F32), ALU.subtract).then_inc(v_utlo, 1)
                if 0 <= k_of(k, -2) < TILES:
                    dve.wait_ge(p_y, k - 1)
                    row = rows[:, bass.ds(k - 2, 1), :].squeeze(1) if not isinstance(k, int) else rows[:, k - 2, :]
                    dve.scalar_tensor_tensor(row[:, 0:D], ps_y[:, 0:D], row[:, PROB:PROB + 1], row[:, 0:D],
                                             ALU.mult, ALU.add).then_inc(v_y, 1)

            run_steps(dve, step, -2)

        @block.tensor
        def _(pe):
            ident = cst[:, C_ID:C_ID + P]
            pe.wait_ge(l_const, 16)
            pe.wait_ge(l_small, 48)
            pe.matmul(ps_l[:, 0:E], cst[:, C_CEN:C_CEN + P], rw[:], start=True, stop=True).then_inc(p_rwc, 1)

            def head(g):
                pe.wait_ge(l_x[g], 16)
                if g >= 1:
                    pe.wait_ge(a_xt, g)
                for j in range(GB):
                    last = pe.transpose(ps_xt[:, j * S:(j + 1) * S], xs[:, GB * g + j, :], ident)
                last.then_inc(p_xt, 1)
                pe.wait_ge(l_ctxt[g % 2], 16 * (g // 2 + 1))
                if g >= 1:
                    pe.wait_ge(a_cc, g)
                pe.matmul(ps_cc[:, 0:GB * K], cst[:, C_CEN:C_CEN + P], ctxt[:, g % 2, :], start=True, stop=True).then_inc(p_cc, 1)

            def scores(g):
                pe.wait_ge(a_xt, g + 1)
                pe.wait_ge(a_cc, g + 1)
                if g >= 2:
                    pe.wait_ge(a_exp, GB * (g - 1))
                for j in range(GB):
                    last = pe.matmul(ps_s[g % 2][:, j * K:(j + 1) * K], xt[:, g % 2, j * S:(j + 1) * S],
                                     ctxc[:, g % 2, j * K:(j + 1) * K], start=True, stop=True)
                last.then_inc(p_s, 1)

            def merge(g):
                pe.wait_ge(v_att, g + 1)
                if g >= 1:
                    pe.wait_ge(a_g, g)
                for j in range(GB):
                    last = pe.matmul(ps_g[0:K, j * D:(j + 1) * D], att[:, g % 2, j, :], wt[:], start=True, stop=True)
                last.then_inc(p_g, 1)

            def output(g):
                pe.wait_ge(a_g, g + 1)
                pe.wait_ge(l_ctxk[g % 2], 16 * (g // 2 + 1))
                if g == 0:
                    pe.wait_ge(l_ones, 16 * 2 * (GB + 1))
                if g >= 1:
                    pe.wait_ge(v_x1, g)
                for j in range(GB):
                    last = pe.matmul(ps_o[:, j * D:(j + 1) * D], ctxk[:, g % 2, j * D:(j + 1) * D],
                                     merged[:, g % 2, j * D:(j + 1) * D], start=True, stop=True)
                last.then_inc(p_o, 1)

            def turn(g):
                pe.wait_ge(v_x1, g + 1)
                if g >= 1:
                    pe.wait_ge(a_x1t, g)
                for j in range(GB):
                    last = pe.transpose(ps_x1t[:, j * S:(j + 1) * S], x1[:, GB * g + j, 0:D], ident)
                last.then_inc(p_x1t, 1)

            def route(g):
                pe.wait_ge(a_x1t, g + 1)
                pe.wait_ge(v_rwc, 1)
                if g >= 1:
                    pe.wait_ge(v_lg0, g)
                for j in range(GB):
                    last = pe.matmul(ps_l[:, j * E:(j + 1) * E], x1t[:, g % 2, j * S:(j + 1) * S], rwc[:], start=True, stop=True)
                last.then_inc(p_l, 1)

            for k in range(NG + 3):
                if 0 <= k - 2 < NG:
                    merge(k - 2)
                if k < NG:
                    head(k)
                if 0 <= k - 3 < NG:
                    turn(k - 3)
                if 0 <= k - 2 < NG:
                    output(k - 2)
                if k < NG:
                    scores(k)
                if 0 <= k - 3 < NG:
                    route(k - 3)

            pe.wait_ge(v_bf, 3)
            pe.wait_ge(v_hot, NG)
            pe.matmul(ps_rank[:, 0:E * B], tri[:], onehot[:].rearrange("p e b -> p (e b)"), start=True, stop=True)
            pe.matmul(ps_cnt[:, 0:E * B], ones[:], onehot[:].rearrange("p e b -> p (e b)"), start=True, stop=True).then_inc(p_rank, 1)
            pe.wait_ge(v_am, 1)
            for b in range(B):
                if b < B - BPOOL:
                    pe.wait_ge(v_bm, b // BSTEP + 1)
                else:
                    pe.wait_ge(g_bm, b - (B - BPOOL) + 1)
                last = pe.matmul(ps_inv[:, 0:TPAD], bmat[:, b, :], amat[:, b, :], start=(b == 0), stop=(b == B - 1))
            last.then_inc(p_inv, 1)
            pe.wait_ge(v_te, 1)
            pe.wait_ge(a_whi, NWP)
            pe.wait_ge(g_wlo, NWP)
            pe.wait_ge(v_sca, 1)

            def step(k, odd=0):
                q = (odd + 1) % 2

                def expert(t):
                    at = tile_expert[0:1, t:t + 1] if isinstance(t, int) else tile_expert[0:1, bass.ds(t, 1)]
                    return pe.value_load(at, min_val=0, max_val=E - 1)

                if 0 <= k_of(k, 1) < TILES:
                    pe.wait_ge(v_hg, k + 2)
                    if k_of(k, 1) >= 1:
                        pe.wait_ge(v_htlo, k + 1)
                    pe.transpose(ps_ht[:, 0:P], hg[:, q, :], ident).then_inc(p_ht, 1)
                if 0 <= k_of(k, 0) < TILES:
                    e = expert(k)
                    pe.wait_ge(a_hthi, k + 1)
                    pe.wait_ge(v_htlo, k + 1)
                    if k_of(k, 0) >= 2:
                        pe.wait_ge(v_u, k - 1)
                    for c, ps, done in ((0, ps_a[odd], p_a), (1, ps_g3[odd], p_gg)):
                        whi = w1hi[:, bass.ds(e * (2 * F) + c * F, F)]
                        wlo = w1lo[:, bass.ds(e * (2 * F) + c * F, F)]
                        pe.matmul(ps[:, :], hthi[:, odd, :], whi, start=True, stop=False)
                        pe.matmul(ps[:, :], hthi[:, odd, :], wlo, start=False, stop=False)
                        pe.matmul(ps[:, :], htlo[:, odd, :], whi, start=False, stop=True).then_inc(done, 1)
                if 0 <= k_of(k, -1) < TILES:
                    pe.wait_ge(v_u, k)
                    if k_of(k, -1) >= 2:
                        pe.wait_ge(v_utlo, k - 2)
                    for c in range(FC):
                        last = pe.transpose(ps_ut[q][:, c * P:(c + 1) * P], u[:, q, c * P:(c + 1) * P], ident)
                    last.then_inc(p_ut, 1)
                if 0 <= k_of(k, -2) < TILES:
                    e = expert(k - 2)
                    pe.wait_ge(a_uthi, k - 1)
                    pe.wait_ge(v_utlo, k - 1)
                    if k_of(k, -2) >= 1:
                        pe.wait_ge(v_y, k - 2)
                    for c in range(FC):
                        whi = w2hi[:, bass.ds(e * (FC * D) + c * D, D)]
                        wlo = w2lo[:, bass.ds(e * (FC * D) + c * D, D)]
                        hi, lo = uthi[:, odd, c * P:(c + 1) * P], utlo[:, odd, c * P:(c + 1) * P]
                        pe.matmul(ps_y[:, 0:D], hi, whi, start=(c == 0), stop=False)
                        pe.matmul(ps_y[:, 0:D], hi, wlo, start=False, stop=False)
                        last = pe.matmul(ps_y[:, 0:D], lo, whi, start=False, stop=(c == FC - 1))
                    last.then_inc(p_y, 1)

            run_steps(pe, step, -1)


def kernel(x, ctx_1024, mask_BxSxS2_bk1, L0_xattn_W_merge, L0_xattn_b_merge, L0_ffn_router_w, L0_ffn_router_b,
           L0_ffn_w1, L0_ffn_w2):
    import concourse.bacc as bacc
    from concourse.bass_utils import run_bass_kernel_spmd

    a = np.ascontiguousarray
    ctx = np.asarray(ctx_1024)
    ins = {
        "x": a(np.asarray(x).transpose(1, 0, 2)),
        "ctx_k": a(ctx.transpose(1, 0, 2).reshape(K, B * D)),
        "ctx_t": a(ctx.transpose(2, 0, 1).reshape(D, B * K)),
        "ctx_one": np.ones((1, GB * D), np.float32),
        "mask": a(np.asarray(mask_BxSxS2_bk1).transpose(1, 0, 2).reshape(S, B * K)),
        "w_t": a(np.asarray(L0_xattn_W_merge).T),
        "b_merge": a(np.asarray(L0_xattn_b_merge).reshape(1, D)),
        "router_w": a(np.asarray(L0_ffn_router_w)),
        "router_b": a(np.asarray(L0_ffn_router_b)),
        "w1": a(np.asarray(L0_ffn_w1).transpose(1, 0, 2).reshape(D, E * 2 * F)),
        "w2": a(np.asarray(L0_ffn_w2).reshape(E, FC, P, D).transpose(2, 0, 1, 3).reshape(P, E * FC * D)),
        "const": constants(),
    }
    nc = bacc.Bacc("TRN2", target_bir_lowering=False, num_devices=1)
    args = {n: nc.dram_tensor(f"in_{n}", v.shape, mybir.dt.from_np(v.dtype), kind="ExternalInput").ap() for n, v in ins.items()}
    out = nc.dram_tensor("out_rows", (TOKENS, D), F32, kind="ExternalOutput").ap()
    build(nc, out=out, **args)
    r = run_bass_kernel_spmd(nc, [{f"in_{n}": v for n, v in ins.items()}], core_ids=[0])
    return r.results[0]["out_rows"].reshape(S, B, D).transpose(1, 0, 2)
```

```python
from contextlib import ExitStack

import numpy as np
import concourse.bass as bass
from concourse import mybir

ALU = mybir.AluOpType
ACT = mybir.ActivationFunctionType
AX = mybir.AxisListType
F32 = mybir.dt.float32
F32R = mybir.dt.float32r
BF16 = mybir.dt.bfloat16
I32 = mybir.dt.int32
U32 = mybir.dt.uint32

P = 128
B, S, D = 32, 128, 128
K = 77
E, F = 8, 512
TOKENS = B * S
GB = 4
NG = B // GB
TILES = TOKENS // P + E - 1
AHEAD = 8
NQ = 4
TPAD = TILES + TILES % 2
GW = D + E
SW = K + E
ROW = D + 4
MEAN, RSTD, PROB = D, D + 1, D + 2
FC = F // P
WCH = 512
NWP = E * 2 * F // WCH
WQ = NWP // 4
BSTEP = 8
SCALE = float(1.0 / np.sqrt(np.float32(D)))
NEG = -1.0e9
EPS = 1.0e-5
ROUND = 1.5 * 2.0 ** 23
EARLY = 8
FAR = 2 * TOKENS

C_ID, C_CEN, C_TRI, C_IOTA = 0, P, 2 * P, 3 * P
C_BAT = 4 * P
C_PB = C_BAT + B
C_KEEP = C_PB + 1
C_EM = C_KEEP + B * E
C_ONE = C_EM + E
C_ALL = C_ONE + E


def constants():
    c = np.zeros((P, C_ALL), np.float32)
    c[:, C_ID:C_ID + P] = np.eye(P)
    c[:, C_CEN:C_CEN + P] = np.eye(P) - 1.0 / P
    c[:, C_TRI:C_TRI + P] = np.triu(np.ones((P, P)), 1)
    c[:, C_IOTA:C_IOTA + P] = np.arange(P)
    c[:, C_BAT:C_BAT + B] = np.arange(B) + 1
    c[:, C_PB] = np.arange(P) * B
    c[:, C_KEEP:C_KEEP + B * E] = np.tile(np.arange(B) > 0, E)
    c[:, C_EM:C_EM + E] = np.arange(E) - E
    c[:, C_ONE:C_ONE + E] = 1.0
    return c


def build(nc, x, ctx_k, ctx_t, ctx_one, mask, w_t, w_n, b_row, b_col, router_w, router_b, w1, w2, const, out):
    x1_rows = nc.dram_tensor("x1_rows", (TOKENS, ROW), F32, kind="Internal").ap()

    with ExitStack() as keep:
        def sb(name, shape, dt=F32, stack=keep):
            return stack.enter_context(nc.sbuf_tensor(name, shape, dt))

        def sem(name):
            return keep.enter_context(nc.semaphore(name))

        cst = sb("cst", [P, C_ALL])
        w1hi = sb("w1hi", [P, E * 2 * F], F32R)
        w1lo = sb("w1lo", [P, E * 2 * F], F32R)
        w2s = sb("w2s", [P, E * FC * D])
        x1 = sb("x1", [P, B, ROW])
        onehot = sb("onehot", [P, E, B], BF16)
        tri = sb("tri", [P, P], BF16)
        ones = sb("ones", [P, P], BF16)
        numbers = sb("numbers", [P, P, B], BF16)
        batno = sb("batno", [P, B], BF16)
        gather_at = sb("gather_at", [P, TPAD], U32)
        scatter_at = sb("scatter_at", [P, TPAD], U32)
        tile_expert = sb("tile_expert", [P, TPAD], I32)

        early = ExitStack()
        xs = sb("xs", [P, B, D], F32, early)
        ctxk = sb("ctxk", [K + 1, B * D], F32, early)
        ctxt = sb("ctxt", [P, B * K], F32, early)
        ctxc = sb("ctxc", [P, 2, GB, SW], F32, early)
        msk = sb("msk", [P, B * K], mybir.dt.uint8, early)
        wt = sb("wt", [P, GW], F32, early)
        wn = sb("wn", [P, D], F32, early)
        bcol = sb("bcol", [P, 1], F32, early)
        bcols = sb("bcols", [P, P], F32, early)
        brw = sb("brw", [P, E], F32, early)
        xrw = sb("xrw", [P, B, E], F32, early)
        rw = sb("rw", [P, E], F32, early)
        rwc = sb("rwc", [P, E], F32, early)
        rb = sb("rb", [P, E], F32, early)
        xt = sb("xt", [P, 2, GB * S], F32, early)
        prob = sb("prob", [P, 2, GB, K], F32, early)
        att = sb("att", [P, 2, GB, K], F32, early)
        merged = sb("merged", [K + 1, 2, GB * GW], F32, early)
        bn = sb("bn", [P, 2, GB, 6], F32, early)
        mv = sb("mv", [P, B, 2], F32, early)
        half = sb("half", [P, GB], F32, early)
        ve = sb("ve", [P, B], F32, early)
        rstd = sb("rstd", [P, B], F32, early)
        rs = sb("rs", [P, B], F32, early)
        fill = sb("fill", [P, B], F32, early)
        nmax = sb("nmax", [P, B], F32, early)
        nbias = sb("nbias", [P, B], F32, early)
        esum = sb("esum", [P, B], F32, early)
        einv = sb("einv", [P, B], F32, early)
        ve2 = sb("ve2", [P, B], F32, early)
        lg0 = sb("lg0", [P, B, E], F32, early)
        lg1 = sb("lg1", [P, B, E], F32, early)
        lg = sb("lg", [P, B, E], F32, early)
        lmax = sb("lmax", [P, B], F32, early)
        ldif = sb("ldif", [P, B, E], F32, early)
        lexp = sb("lexp", [P, B, E], F32, early)
        lsum = sb("lsum", [P, B], F32, early)
        cand = sb("cand", [P, B, E], F32, early)
        emin = sb("emin", [P, B], F32, early)
        wraw = sb("wraw", [P, 3 * WQ * WCH], F32, early)
        early.close()

        late = keep
        pre = sb("pre", [P, E, B])
        tl0 = sb("tl0", [P, E])
        tl = sb("tl", [P, E])
        tend = sb("tend", [P, E])
        tbeg = sb("tbeg", [P, E])
        sl0 = sb("sl0", [P, E, B])
        sl1 = sb("sl1", [P, E, B])
        sl2 = sb("sl2", [P, E, B])
        sl3 = sb("sl3", [P, E, B])
        slot = sb("slot", [P, B])
        jt0 = sb("jt0", [P, B])
        jt = sb("jt", [P, B], BF16)
        rm = sb("rm", [P, B], BF16)
        tcmp = sb("tcmp", [P, TPAD, E])
        tcnt = sb("tcnt", [P, TPAD])
        inv0 = sb("inv0", [P, TPAD])
        inv = sb("inv", [P, TPAD])
        vz = sb("vz", [P, TPAD])
        a0 = sb("a0", [P, TPAD, B], BF16)
        amat = sb("amat", [P, 2, TPAD, B], BF16)
        bmat = sb("bmat", [P, P, B], BF16)
        rows = sb("rows", [P, TILES, ROW])
        hg = sb("hg", [P, 2, D])
        hthi = sb("hthi", [P, 2, P], F32R)
        htlo = sb("htlo", [P, 2, P], F32R)
        sa = sb("sa", [P, 2, F])
        u = sb("u", [P, 2, F])
        ut = sb("ut", [P, 2, F])

        banks = keep.enter_context(nc.psum_tensor("banks", [P, 8 * 512], F32))
        bank = [banks[:, i * 512:(i + 1) * 512] for i in range(8)]
        ps_xt, ps_cc, ps_s = bank[0], bank[1], bank[2:4]
        ps_g, ps_o = (banks[:, i * 512:(i + 2) * 512].rearrange("p (h c) -> p h c", h=2)[:, :, 0:2 * GW] for i in (4, 6))
        ps_rank, ps_cnt, ps_inv = bank[0], bank[1], bank[2]
        ps_a, ps_g3, ps_ut, ps_ht, ps_y = bank[0:2], bank[2:4], bank[4:6], bank[6], bank[7]

        l_const, l_const2, l_rw, l_merge, l_rb, l_mask, l_ones, l_w2 = (
            sem(n) for n in ("l_const", "l_const2", "l_rw", "l_merge", "l_rb", "l_mask", "l_ones", "l_w2"))
        l_x = [sem(f"l_x{g}") for g in range(NG)]
        l_ctxk = [sem(f"l_ctxk{i}") for i in range(2)]
        l_ctxt = [sem(f"l_ctxt{i}") for i in range(2)]
        l_w1 = [sem(f"l_w1{i}") for i in range(4)]
        s_rows = sem("s_rows")
        p_xt, p_cc, p_s, p_g, p_o = (sem(n) for n in ("p_xt", "p_cc", "p_s", "p_g", "p_o"))
        p_rwc, p_router = sem("p_rwc"), sem("p_router")
        a_xt, a_cc, a_exp, a_g, a_rexp, a_whi, a_num = (sem(n) for n in ("a_xt", "a_cc", "a_exp", "a_g", "a_rexp", "a_whi", "a_num"))
        v_bf, v_rwc, v_router, v_bn, v_mv, v_rs, v_fill, v_mask, v_max, v_nb, v_xrw, v_inv = (
            sem(n) for n in ("v_bf", "v_rwc", "v_router", "v_bn", "v_mv", "v_rs", "v_fill", "v_mask", "v_max", "v_nb", "v_xrw", "v_inv"))
        v_x1, v_bn2, v_mv2, v_lg0, v_lg1, v_lg, v_lmax, v_ldif, v_cand, v_emin, v_hot, v_lsum, v_prob = (
            sem(n) for n in ("v_x1", "v_bn2", "v_mv2", "v_lg0", "v_lg1", "v_lg", "v_lmax", "v_ldif", "v_cand", "v_emin", "v_hot", "v_lsum", "v_prob"))
        g_half, g_bcols, g_ve, g_rstd, g_att, g_ve2, g_rstd2, g_wlo = (
            sem(n) for n in ("g_half", "g_bcols", "g_ve", "g_rstd", "g_att", "g_ve2", "g_rstd2", "g_wlo"))
        p_rank, p_inv = sem("p_rank"), sem("p_inv")
        v_chain = sem("v_chain")
        v_tl0, v_tl, v_sl0, v_sl1, v_tcnt = (sem(n) for n in ("v_tl0", "v_tl", "v_sl0", "v_sl1", "v_tcnt"))
        v_a0, v_am, a_am, v_bm, v_gat, v_sca, v_te = (sem(n) for n in ("v_a0", "v_am", "a_am", "v_bm", "v_gat", "v_sca", "v_te"))
        g_rows = [sem(f"g_rows{i}") for i in range(NQ)]
        g_out = sem("g_out")
        p_ht, p_a, p_gg, p_ut, p_y = (sem(n) for n in ("p_ht", "p_a", "p_gg", "p_ut", "p_y"))
        a_hthi, a_sa, a_ut = sem("a_hthi"), sem("a_sa"), sem("a_ut")
        v_hg, v_htlo, v_u, v_y = sem("v_hg"), sem("v_htlo"), sem("v_u"), sem("v_y")

        def group(t, g):
            return t[:, GB * g:GB * g + GB]

        def wpiece(i):
            r = i % (3 * WQ)
            return [wraw[:, r * WCH:(r + 1) * WCH]] + [w[:, i * WCH:(i + 1) * WCH] for w in (w1hi, w1lo)]

        def stage(g, part):
            if 0 <= g < NG:
                part(g)

        block = keep.enter_context(nc.Block())

        @block.sync
        def _(sp):
            half, quarter = B // 2, NWP * WCH // 4

            def load_ctxt(h):
                cols = slice((0, 2 * GB * K)[h], (2 * GB * K, B * K)[h])
                sp.dma_start(ctxt[:, cols], ctx_t[:, cols]).then_inc(l_ctxt[h], 16)

            def load_ctxk(h):
                sp.dma_start(ctxk[0:K, h * half * D:(h + 1) * half * D], ctx_k[:, h * half * D:(h + 1) * half * D]).then_inc(l_ctxk[h], 16)

            def load_x(g):
                sp.dma_start(group(xs, g), x[:, GB * g:GB * g + GB, :]).then_inc(l_x[g], 16)

            def load_w1(q):
                sp.dma_start(wraw[:, q % 3 * quarter:(q % 3 + 1) * quarter], w1[:, q * quarter:(q + 1) * quarter]).then_inc(l_w1[q], 16)

            load_x(0)
            sp.dma_start(cst[:, 0:C_TRI], const[:, 0:C_TRI]).then_inc(l_const, 16)
            load_ctxt(0)
            sp.dma_start(rw[:], router_w).then_inc(l_rw, 16)
            sp.dma_start(msk[:], mask).then_inc(l_mask, 16)
            load_x(1)
            sp.dma_start(bcol[:], b_col).then_inc(l_merge, 16)
            sp.dma_start(wn[:], w_n).then_inc(l_merge, 16)
            sp.dma_start(wt[:, 0:D], w_t).then_inc(l_merge, 16)
            load_ctxk(0)
            sp.dma_start(ctxk[K:K + 1, :], ctx_one).then_inc(l_ones, 16)
            sp.dma_start(merged[K:K + 1, :, :].rearrange("k i (j d) -> k (i j) d", d=GW),
                         b_row.unsqueeze(1).to_broadcast([1, 2 * GB, GW])).then_inc(l_ones, 16)
            sp.dma_start(cst[:, C_TRI:C_ALL], const[:, C_TRI:C_ALL]).then_inc(l_const2, 16)
            load_x(2)
            sp.dma_start(rb[:], router_b.partition_broadcast(P)).then_inc(l_rb, 16)
            load_ctxt(1)
            load_x(3)
            load_w1(0)
            load_x(4)
            load_x(5)
            load_ctxk(1)
            load_x(6)
            load_x(7)
            load_w1(1)
            load_w1(2)
            sp.dma_start(w2s[:], w2).then_inc(l_w2, 16)
            sp.wait_ge(g_wlo, WQ)
            load_w1(3)
            for g in range(NG):
                sp.wait_ge(v_prob, g + 1)
                sp.wait_ge(g_rstd2, g + 1)
                sp.dma_start(x1_rows.rearrange("(l b) c -> l b c", b=B)[:, GB * g:GB * g + GB, :],
                             group(x1, g)).then_inc(s_rows, 16)

        @block.gpsimd
        def _(pool):
            nc.gpsimd.memset(half[:], -0.5).then_inc(g_half, 1)
            pool.wait_ge(g_half, 1)

            def w_lo(i):
                raw, hi, lo = wpiece(i)
                pool.wait_ge(a_whi, i + 1)
                pool.tensor_tensor(lo, raw, hi.bitcast(F32), ALU.subtract).then_inc(g_wlo, 1)

            def rstd1(g):
                pool.wait_ge(v_mv, g + 1)
                pool.tensor_scalar(group(ve, g), mv[:, GB * g:GB * g + GB, 1], EPS, None, ALU.add).then_inc(g_ve, 1)
                pool.wait_ge(g_ve, g + 1)
                pool.tensor_tensor(group(rstd, g), group(ve, g), half[:], ALU.pow).then_inc(g_rstd, 1)

            def rstd2(g):
                pool.wait_ge(v_mv2, g + 1)
                pool.tensor_scalar(group(ve2, g), x1[:, GB * g:GB * g + GB, RSTD], EPS, None, ALU.add).then_inc(g_ve2, 1)
                pool.wait_ge(g_ve2, g + 1)
                pool.tensor_tensor(x1[:, GB * g:GB * g + GB, RSTD], group(ve2, g), half[:], ALU.pow).then_inc(g_rstd2, 1)

            def weights(g):
                pool.wait_ge(v_inv, g + 1)
                if g >= 2:
                    pool.wait_ge(p_g, g - 1)
                pool.tensor_tensor(att[:, g % 2], prob[:, g % 2], group(einv, g).unsqueeze(2).to_broadcast([P, GB, K]),
                                   ALU.mult).then_inc(g_att, 1)

            pool.wait_ge(l_merge, 48)
            pool.tensor_copy(bcols[:], bcol[:].to_broadcast([P, P])).then_inc(g_bcols, 1)
            for k in range(-1, NG + 4):
                stage(k + 1, rstd1)
                stage(k - 1, weights)
                stage(k - 3, rstd2)
                if 0 <= k - 2 < EARLY:
                    w_lo(k - 2)
            for i in range(EARLY, NWP):
                w_lo(i)

            def gather(i):
                if i == 0:
                    pool.wait_ge(v_gat, 1)
                    pool.wait_ge(s_rows, 16 * NG)
                if i >= NQ:
                    pool.wait_ge(g_rows[i % NQ], 16 * (i // NQ))
                pool.indirect_dma_start(rows[:, i, :], None, x1_rows,
                                        bass.IndirectOffsetOnAxis(gather_at[:, i:i + 1], 0)).then_inc(g_rows[i % NQ], 16)

            def scatter(i):
                if i == 0:
                    pool.wait_ge(v_sca, 1)
                pool.wait_ge(v_y, i + 1)
                pool.indirect_dma_start(out, bass.IndirectOffsetOnAxis(scatter_at[:, i:i + 1], 0), rows[:, i, 0:D], None,
                                        bounds_check=TOKENS - 1, oob_is_err=False).then_inc(g_out, 16)

            for i in range(TILES + AHEAD):
                if i < TILES:
                    gather(i)
                if i >= AHEAD:
                    scatter(i - AHEAD)
            pool.wait_ge(g_out, 16 * TILES)

        @block.scalar
        def _(act):
            def w_hi(i):
                raw, hi, _ = wpiece(i)
                act.wait_ge(l_w1[i // WQ], 16)
                act.activation(hi, raw, ACT.Copy).then_inc(a_whi, 1)

            def copy_xt(g):
                act.wait_ge(p_xt, g + 1)
                if g >= 2:
                    act.wait_ge(p_s, g - 1)
                act.activation(xt[:, g % 2, :], ps_xt[:, :], ACT.Copy).then_inc(a_xt, 1)

            def copy_ctx(g):
                act.wait_ge(p_cc, g + 1)
                act.activation(ctxc[:, g % 2, :, 0:K], ps_cc[:, 0:GB * K].rearrange("p (b k) -> p b k", b=GB),
                               ACT.Copy).then_inc(a_cc, 1)

            def copy_merged(g):
                act.wait_ge(p_g, g + 1)
                if g >= 2:
                    act.wait_ge(p_o, g - 1)
                act.activation(merged[0:K, g % 2, :].rearrange("k (h c) -> k h c", h=2), ps_g[0:K], ACT.Copy).then_inc(a_g, 1)

            def exponentials(g):
                act.wait_ge(v_nb, g + 1)
                if g >= 2:
                    act.wait_ge(g_att, g - 1)
                for j in range(GB):
                    b = GB * g + j
                    act.activation(prob[:, g % 2, j, :], ps_s[g % 2][:, j * SW:j * SW + K], ACT.Exp,
                                   bias=nbias[:, b:b + 1], scale=rs[:, b:b + 1],
                                   accum_out=esum[:, b:b + 1]).then_inc(a_exp, 1)

            def router_exponentials(g):
                act.wait_ge(v_ldif, g + 1)
                act.activation(group(lexp, g), group(ldif, g), ACT.Exp).then_inc(a_rexp, 1)

            for k in range(NG + 5):
                stage(k - 4, router_exponentials)
                stage(k, copy_xt)
                stage(k, copy_ctx)
                stage(k - 2, copy_merged)
                if 0 <= k - 2 < EARLY:
                    w_hi(k - 2)
                if 1 <= k < 5:
                    if k == 1:
                        act.wait_ge(l_const2, 16)
                    r = (k - 1) * (P // 4)
                    act.activation(numbers[:, r:r + P // 4, :], cst[:, C_IOTA + r:C_IOTA + r + P // 4].unsqueeze(2).to_broadcast([P, P // 4, B]),
                                   ACT.Copy).then_inc(a_num, 1)
                stage(k - 0, exponentials)

            for i in range(EARLY, NWP - 2):
                w_hi(i)
            act.wait_ge(v_a0, 1)
            act.activation(amat[:, 0, :, :], a0[:], ACT.Copy, scale=cst[:, C_PB:C_PB + 1]).then_inc(a_am, 1)
            for i in range(NWP - 2, NWP):
                w_hi(i)

            def step(k, odd=0):
                if 0 <= k + 1 < TILES:
                    q = (odd + 1) % 2
                    act.wait_ge(p_ht, k + 2)
                    if k + 1 >= 2:
                        act.wait_ge(p_gg, k)
                    act.activation(hthi[:, q, :], ps_ht[:, 0:P], ACT.Copy).then_inc(a_hthi, 1)
                if 0 <= k < TILES:
                    act.wait_ge(p_a, k + 1)
                    if k >= 2:
                        act.wait_ge(v_u, k - 1)
                    act.activation(sa[:, odd, :], ps_a[odd][:, :], ACT.Silu).then_inc(a_sa, 1)
                if 0 <= k - 1 < TILES:
                    q = (odd + 1) % 2
                    act.wait_ge(p_ut, k)
                    if k - 1 >= 2:
                        act.wait_ge(p_y, k - 2)
                    act.activation(ut[:, q, :], ps_ut[q][:, :], ACT.Copy).then_inc(a_ut, 1)

            for k in range(-1, TILES + 2):
                step(k, odd=k % 2)

        @block.vector
        def _(dve):
            def stats1(g):
                dve.wait_ge(l_x[g], 16)
                if g >= 1:
                    dve.wait_ge(v_mv, g)
                for j in range(GB):
                    dve.bn_stats(bn[:, 0, j, :], xs[:, GB * g + j, :]).then_inc(v_bn, 1)

            def mean1(g):
                dve.wait_ge(v_bn, GB * (g + 1))
                for j in range(GB):
                    last = dve.bn_aggr(mv[:, GB * g + j, :], bn[:, 0, j, :])
                last.then_inc(v_mv, 1)

            def scales(g):
                dve.wait_ge(g_rstd, g + 1)
                dve.tensor_scalar(group(rs, g), group(rstd, g), SCALE, None, ALU.mult).then_inc(v_rs, 1)
                dve.scalar_tensor_tensor(group(fill, g), group(ve, g), NEG / SCALE, group(rstd, g), ALU.mult, ALU.mult).then_inc(v_fill, 1)

            def batches(t, g):
                return t[g % 2][:, 0:GB * SW].rearrange("p (b k) -> p b k", b=GB)

            def x_router(g):
                dve.wait_ge(p_s, g + 1)
                dve.tensor_tensor(group(xrw, g), batches(ps_s, g)[:, :, K:SW], brw[:].unsqueeze(1).to_broadcast([P, GB, E]),
                                  ALU.add).then_inc(v_xrw, 1)

            def fill_masked(g):
                dve.wait_ge(v_fill, g + 1)
                if g == 0:
                    dve.wait_ge(l_mask, 16)
                dve.copy_predicated(batches(ps_s, g)[:, :, 0:K], msk[:, g * GB * K:(g + 1) * GB * K].rearrange("p (b k) -> p b k", b=GB),
                                    group(fill, g).unsqueeze(2).to_broadcast([P, GB, K])).then_inc(v_mask, 1)

            def maximum(g):
                dve.wait_ge(v_mask, g + 1)
                dve.tensor_reduce(group(nmax, g), batches(ps_s, g)[:, :, 0:K], AX.X, ALU.max, negate=True).then_inc(v_max, 1)

            def exp_bias(g):
                dve.wait_ge(v_max, g + 1)
                dve.wait_ge(v_rs, g + 1)
                dve.tensor_tensor(group(nbias, g), group(nmax, g), group(rs, g), ALU.mult).then_inc(v_nb, 1)

            def inverse_sum(g):
                dve.wait_ge(a_exp, GB * (g + 1))
                dve.reciprocal(group(einv, g), group(esum, g)).then_inc(v_inv, 1)

            halves = ps_o.rearrange("p h (b c) -> p h b c", b=2)

            def residual(g):
                dve.wait_ge(p_o, g + 1)
                dve.tensor_tensor(x1[:, GB * g:GB * g + GB, 0:D].rearrange("p (h b) d -> p h b d", h=2), halves[:, :, :, 0:D],
                                  group(xs, g).rearrange("p (h b) d -> p h b d", h=2), ALU.add).then_inc(v_x1, 1)

            def stats2(g):
                dve.wait_ge(v_x1, g + 1)
                if g >= 1:
                    dve.wait_ge(v_mv2, g)
                for j in range(GB):
                    dve.bn_stats(bn[:, 1, j, :], x1[:, GB * g + j, 0:D]).then_inc(v_bn2, 1)

            def mean2(g):
                dve.wait_ge(v_bn2, GB * (g + 1))
                for j in range(GB):
                    last = dve.bn_aggr(x1[:, GB * g + j, MEAN:RSTD + 1], bn[:, 1, j, :])
                last.then_inc(v_mv2, 1)

            wide = [P, GB, E]

            def logits0(g):
                dve.wait_ge(p_o, g + 1)
                dve.wait_ge(v_xrw, g + 1)
                dve.tensor_tensor(group(lg0, g).rearrange("p (h b) e -> p h b e", h=2), halves[:, :, :, D:GW],
                                  group(xrw, g).rearrange("p (h b) e -> p h b e", h=2), ALU.add).then_inc(v_lg0, 1)

            def logits1(g):
                dve.wait_ge(v_lg0, g + 1)
                dve.wait_ge(g_rstd2, g + 1)
                dve.tensor_tensor(group(lg1, g), group(lg0, g), x1[:, GB * g:GB * g + GB, RSTD].unsqueeze(2).to_broadcast(wide),
                                  ALU.mult).then_inc(v_lg1, 1)

            def logits2(g):
                dve.wait_ge(v_lg1, g + 1)
                if g == 0:
                    dve.wait_ge(l_rb, 16)
                dve.tensor_tensor(group(lg, g), group(lg1, g), rb[:].unsqueeze(1).to_broadcast(wide), ALU.add).then_inc(v_lg, 1)

            def greatest(g):
                dve.wait_ge(v_lg, g + 1)
                dve.tensor_reduce(group(lmax, g), group(lg, g), AX.X, ALU.max).then_inc(v_lmax, 1)

            def differences(g):
                dve.wait_ge(v_lmax, g + 1)
                dve.tensor_tensor(group(ldif, g), group(lg, g), group(lmax, g).unsqueeze(2).to_broadcast(wide), ALU.subtract).then_inc(v_ldif, 1)

            def candidates(g):
                dve.wait_ge(v_ldif, g + 1)
                dve.scalar_tensor_tensor(group(cand, g), group(ldif, g), 0.0,
                                         cst[:, C_EM:C_EM + E].unsqueeze(1).to_broadcast(wide), ALU.is_ge, ALU.mult).then_inc(v_cand, 1)

            def first(g):
                dve.wait_ge(v_cand, g + 1)
                dve.tensor_reduce(group(emin, g), group(cand, g), AX.X, ALU.min).then_inc(v_emin, 1)

            def choice(g):
                dve.wait_ge(v_emin, g + 1)
                dve.tensor_tensor(onehot[:, :, GB * g:GB * g + GB].rearrange("p e b -> p b e"), cst[:, C_EM:C_EM + E].unsqueeze(1).to_broadcast(wide),
                                  group(emin, g).unsqueeze(2).to_broadcast(wide), ALU.is_equal).then_inc(v_hot, 1)

            def router_sum(g):
                dve.wait_ge(a_rexp, g + 1)
                dve.tensor_reduce(group(lsum, g), group(lexp, g), AX.X, ALU.add).then_inc(v_lsum, 1)

            def probability(g):
                dve.wait_ge(v_lsum, g + 1)
                dve.reciprocal(x1[:, GB * g:GB * g + GB, PROB], group(lsum, g)).then_inc(v_prob, 1)

            dve.memset(x1[:, :, PROB + 1:ROW], 0.0).then_inc(v_bf, 1)
            dve.memset(ones[:], 1.0).then_inc(v_bf, 1)
            stats1(0)
            dve.wait_ge(p_rwc, 1)
            dve.tensor_copy(rwc[:], ps_g[:, 0, 0:E]).then_inc(v_rwc, 1)
            dve.tensor_copy(ctxc[:, :, :, K:SW].rearrange("p i b e -> p (i b) e"),
                            ps_g[:, 0, 0:E].unsqueeze(1).to_broadcast([P, 2 * GB, E])).then_inc(v_rwc, 1)
            mean1(0)
            stats1(1)
            dve.wait_ge(p_router, 1)
            dve.tensor_copy(wt[:, D:GW], ps_g[:, 1, 0:E]).then_inc(v_router, 1)
            dve.tensor_copy(brw[:], ps_g[:, 1, E:2 * E]).then_inc(v_router, 1)
            mean1(1)
            for k in range(NG + 5):
                if k == 1:
                    dve.wait_ge(l_const2, 16)
                    dve.tensor_copy(tri[:], cst[:, C_TRI:C_TRI + P]).then_inc(v_bf, 1)
                    dve.tensor_copy(batno[:], cst[:, C_BAT:C_BAT + B]).then_inc(v_bf, 1)
                stage(k - 4, greatest)
                stage(k - 1, inverse_sum)
                stage(k - 4, differences)
                stage(k - 3, stats2)
                stage(k - 4, candidates)
                stage(k - 3, mean2)
                stage(k - 4, first)
                stage(k, scales)
                if k == 0:
                    dve.wait_ge(v_router, 2)
                stage(k, x_router)
                stage(k - 4, choice)
                stage(k, fill_masked)
                stage(k - 4, router_sum)
                stage(k, maximum)
                stage(k - 2, logits0)
                stage(k, exp_bias)
                stage(k - 2, residual)
                stage(k - 4, probability)
                stage(k + 2, stats1)
                stage(k - 3, logits1)
                stage(k + 2, mean1)
                stage(k - 3, logits2)

            steps = [0]

            def then(ins):
                steps[0] += 1
                ins.then_inc(v_chain, 1)
                dve.wait_ge(v_chain, steps[0])

            dve.wait_ge(p_rank, 1)
            cnt3 = ps_cnt[:, 0:E * B].rearrange("p (e b) -> p e b", e=E)
            rank3 = ps_rank[:, 0:E * B].rearrange("p (e b) -> p e b", e=E)
            wide = [P, E, B]
            then(dve.tensor_tensor_scan(pre[:].rearrange("p e b -> p (e b)"), cst[:, C_KEEP:C_KEEP + E * B],
                                        ps_cnt[:, 0:E * B], 0.0, ALU.mult, ALU.add))
            dve.tensor_scalar(tl0[:], pre[:, :, B - 1], P / 2 - 0.5, 1.0 / P, ALU.add, ALU.mult).then_inc(v_tl0, 1)
            dve.tensor_tensor(sl0[:], pre[:], cnt3, ALU.subtract).then_inc(v_sl0, 1)
            dve.wait_ge(v_tl0, 1)
            dve.tensor_scalar(tl[:], tl0[:], ROUND, ROUND, ALU.add, ALU.subtract).then_inc(v_tl, 1)
            dve.wait_ge(v_sl0, 1)
            dve.tensor_tensor(sl1[:], sl0[:], rank3, ALU.add).then_inc(v_sl1, 1)
            dve.wait_ge(v_tl, 1)
            then(dve.tensor_tensor_scan(tend[:], cst[:, C_ONE:C_ONE + E], tl[:], 0.0, ALU.mult, ALU.add))
            then(dve.tensor_tensor(tbeg[:], tend[:], tl[:], ALU.subtract))
            dve.wait_ge(v_sl1, 1)
            then(dve.scalar_tensor_tensor(sl2[:], tbeg[:].unsqueeze(2).to_broadcast(wide), float(P), sl1[:], ALU.mult, ALU.add))
            then(dve.tensor_tensor(sl3[:], sl2[:], onehot[:], ALU.mult))
            then(dve.tensor_reduce(slot[:], sl3[:].rearrange("p e b -> p b e"), AX.X, ALU.add))
            then(dve.tensor_scalar(jt0[:], slot[:], -(P / 2 - 0.5), 1.0 / P, ALU.add, ALU.mult))
            then(dve.tensor_scalar(jt[:], jt0[:], ROUND, ROUND, ALU.add, ALU.subtract))
            wide = [P, TPAD, B]
            dve.wait_ge(a_num, 4)
            dve.tensor_tensor(a0[:], numbers[:, 0:TPAD, :], jt[:].unsqueeze(1).to_broadcast(wide), ALU.is_equal).then_inc(v_a0, 1)
            then(dve.scalar_tensor_tensor(rm[:], jt[:], -float(P), slot[:], ALU.mult, ALU.add))
            for b in range(0, B, BSTEP):
                if b == BSTEP:
                    dve.wait_ge(v_a0, 1)
                    dve.tensor_tensor(amat[:, 1, :, :], a0[:], batno[:].unsqueeze(1).to_broadcast(wide), ALU.mult).then_inc(v_am, 1)
                dve.tensor_tensor(bmat[:, :, b:b + BSTEP], numbers[:, :, b:b + BSTEP],
                                  rm[:, b:b + BSTEP].unsqueeze(1).to_broadcast([P, P, BSTEP]), ALU.is_equal).then_inc(v_bm, 1)
            wide = [P, TPAD, E]
            then(dve.tensor_tensor(tcmp[:], tend[:].unsqueeze(1).to_broadcast(wide),
                                   cst[:, C_IOTA:C_IOTA + TPAD].unsqueeze(2).to_broadcast(wide), ALU.is_le))
            dve.tensor_reduce(tcnt[:], tcmp[:], AX.X, ALU.add).then_inc(v_tcnt, 1)
            dve.wait_ge(p_inv, 1)
            then(dve.tensor_copy(inv0[:], ps_inv[:, 0:TPAD]))
            then(dve.tensor_tensor(inv[:], ps_inv[:, TPAD:2 * TPAD], inv0[:], ALU.add))
            dve.tensor_scalar(gather_at[:], inv[:], 1.0, 1.0, ALU.max, ALU.subtract).then_inc(v_gat, 1)
            dve.wait_ge(v_tcnt, 1)
            dve.tensor_scalar(tile_expert[:], tcnt[:], float(E - 1), None, ALU.min).then_inc(v_te, 1)
            then(dve.tensor_scalar(vz[:], inv[:], 0.0, float(FAR + 1), ALU.is_equal, ALU.mult))
            dve.scalar_tensor_tensor(scatter_at[:], inv[:], -1.0, vz[:], ALU.add, ALU.add).then_inc(v_sca, 1)

            def step(k, odd=0):
                q = (odd + 1) % 2
                if 0 <= k + 2 < TILES:
                    dve.wait_ge(g_rows[(k + 2) % NQ], 16 * ((k + 2) // NQ + 1))
                    if k + 2 >= 2:
                        dve.wait_ge(p_ht, k + 1)
                    row = rows[:, k + 2, :]
                    dve.tensor_scalar(hg[:, odd, :], row[:, 0:D], row[:, MEAN:MEAN + 1], row[:, RSTD:RSTD + 1],
                                      ALU.subtract, ALU.mult).then_inc(v_hg, 1)
                if 0 <= k + 1 < TILES:
                    dve.wait_ge(a_hthi, k + 2)
                    if k + 1 >= 2:
                        dve.wait_ge(p_gg, k)
                    dve.tensor_tensor(htlo[:, q, :], ps_ht[:, 0:P], hthi[:, q, :].bitcast(F32), ALU.subtract).then_inc(v_htlo, 1)
                if 0 <= k < TILES:
                    dve.wait_ge(p_gg, k + 1)
                    dve.wait_ge(a_sa, k + 1)
                    if k >= 2:
                        dve.wait_ge(p_ut, k - 1)
                    dve.tensor_tensor(u[:, odd, :], ps_g3[odd][:, :], sa[:, odd, :], ALU.mult).then_inc(v_u, 1)
                if 0 <= k - 2 < TILES:
                    dve.wait_ge(p_y, k - 1)
                    row = rows[:, k - 2, :]
                    dve.scalar_tensor_tensor(row[:, 0:D], ps_y[:, 0:D], row[:, PROB:PROB + 1], row[:, 0:D],
                                             ALU.mult, ALU.add).then_inc(v_y, 1)

            for k in range(-2, TILES + 2):
                step(k, odd=k % 2)

        @block.tensor
        def _(pe):
            ident = cst[:, C_ID:C_ID + P]
            centre = cst[:, C_CEN:C_CEN + P]

            def turn_x(g):
                if g == 0:
                    pe.wait_ge(l_const, 16)
                pe.wait_ge(l_x[g], 16)
                if g >= 1:
                    pe.wait_ge(a_xt, g)
                for j in range(GB):
                    last = pe.transpose(ps_xt[:, j * S:(j + 1) * S], xs[:, GB * g + j, :], ident)
                last.then_inc(p_xt, 1)

            def centre_ctx(g):
                pe.wait_ge(l_ctxt[0 if g < 2 else 1], 16)
                if g >= 1:
                    pe.wait_ge(a_cc, g)
                pe.matmul(ps_cc[:, 0:GB * K], centre, ctxt[:, g * GB * K:(g + 1) * GB * K], start=True, stop=True).then_inc(p_cc, 1)

            def scores(g):
                pe.wait_ge(a_xt, g + 1)
                pe.wait_ge(a_cc, g + 1)
                if g == 0:
                    pe.wait_ge(v_rwc, 2)
                if g >= 2:
                    pe.wait_ge(a_exp, GB * (g - 1))
                for j in range(GB):
                    last = pe.matmul(ps_s[g % 2][:, j * SW:(j + 1) * SW], xt[:, g % 2, j * S:(j + 1) * S],
                                     ctxc[:, g % 2, j, :], start=True, stop=True)
                last.then_inc(p_s, 1)

            def merge(g):
                pe.wait_ge(g_att, g + 1)
                if g == 0:
                    pe.wait_ge(v_router, 2)
                if g >= 1:
                    pe.wait_ge(a_g, g)
                for j in range(GB):
                    last = pe.matmul(ps_g[0:K, j // 2, j % 2 * GW:(j % 2 + 1) * GW], att[:, g % 2, j, :], wt[:], start=True, stop=True)
                last.then_inc(p_g, 1)

            def output(g):
                pe.wait_ge(a_g, g + 1)
                pe.wait_ge(l_ctxk[g * 2 // NG], 16)
                if g == 0:
                    pe.wait_ge(l_ones, 32)
                if g >= 1:
                    pe.wait_ge(v_x1, g)
                    pe.wait_ge(v_lg0, g)
                for j in range(GB):
                    last = pe.matmul(ps_o[:, j // 2, j % 2 * GW:(j % 2 + 1) * GW], ctxk[:, (GB * g + j) * D:(GB * g + j + 1) * D],
                                     merged[:, g % 2, j * GW:(j + 1) * GW], start=True, stop=True)
                last.then_inc(p_o, 1)

            turn_x(0)
            pe.wait_ge(l_rw, 16)
            pe.matmul(ps_g[:, 0, 0:E], centre, rw[:], start=True, stop=True).then_inc(p_rwc, 1)
            centre_ctx(0)
            pe.wait_ge(v_rwc, 1)
            pe.wait_ge(l_merge, 48)
            pe.matmul(ps_g[:, 1, 0:E], wn[:], rwc[:], start=True, stop=True)
            pe.wait_ge(g_bcols, 1)
            pe.matmul(ps_g[:, 1, E:2 * E], bcols[:], rwc[:], start=True, stop=True).then_inc(p_router, 1)
            for k in range(NG + 3):
                if k > 0:
                    stage(k, turn_x)
                    stage(k, centre_ctx)
                stage(k, scores)
                stage(k - 2, output)
                stage(k - 1, merge)

            pe.wait_ge(v_bf, 4)
            pe.wait_ge(v_hot, NG)
            pe.matmul(ps_rank[:, 0:E * B], tri[:], onehot[:].rearrange("p e b -> p (e b)"), start=True, stop=True)
            pe.matmul(ps_cnt[:, 0:E * B], ones[:], onehot[:].rearrange("p e b -> p (e b)"), start=True, stop=True).then_inc(p_rank, 1)
            pe.wait_ge(v_am, 1)
            pe.wait_ge(a_am, 1)
            for b in range(B):
                pe.wait_ge(v_bm, b // BSTEP + 1)
                last = pe.matmul(ps_inv[:, 0:2 * TPAD], bmat[:, :, b], amat[:, :, :, b], start=(b == 0), stop=(b == B - 1))
            last.then_inc(p_inv, 1)
            pe.wait_ge(v_te, 1)
            pe.wait_ge(a_whi, NWP)
            pe.wait_ge(g_wlo, NWP)
            pe.wait_ge(l_w2, 16)
            pe.wait_ge(v_sca, 1)

            experts = {}

            def step(k, odd=0):
                q = (odd + 1) % 2
                if 0 <= k + 1 < TILES:
                    pe.wait_ge(v_hg, k + 2)
                    if k + 1 >= 1:
                        pe.wait_ge(v_htlo, k + 1)
                    pe.transpose(ps_ht[:, 0:P], hg[:, q, :], ident).then_inc(p_ht, 1)
                if 0 <= k < TILES:
                    e = experts[k] = pe.value_load(tile_expert[0:1, k:k + 1], min_val=0, max_val=E - 1)
                    pe.wait_ge(a_hthi, k + 1)
                    pe.wait_ge(v_htlo, k + 1)
                    if k >= 2:
                        pe.wait_ge(v_u, k - 1)
                    for c, ps, done in ((0, ps_a[odd], p_a), (1, ps_g3[odd], p_gg)):
                        whi = w1hi[:, bass.ds(e * (2 * F) + c * F, F)]
                        wlo = w1lo[:, bass.ds(e * (2 * F) + c * F, F)]
                        pe.matmul(ps[:, :], hthi[:, odd, :], whi, start=True, stop=False)
                        pe.matmul(ps[:, :], hthi[:, odd, :], wlo, start=False, stop=False)
                        pe.matmul(ps[:, :], htlo[:, odd, :], whi, start=False, stop=True).then_inc(done, 1)
                if 0 <= k - 1 < TILES:
                    pe.wait_ge(v_u, k)
                    if k - 1 >= 2:
                        pe.wait_ge(a_ut, k - 2)
                    for c in range(FC):
                        last = pe.transpose(ps_ut[q][:, c * P:(c + 1) * P], u[:, q, c * P:(c + 1) * P], ident)
                    last.then_inc(p_ut, 1)
                if 0 <= k - 2 < TILES:
                    pe.wait_ge(a_ut, k - 1)
                    if k - 2 >= 1:
                        pe.wait_ge(v_y, k - 2)
                    e = experts[k - 2]
                    for c in range(FC):
                        last = pe.matmul(ps_y[:, 0:D], ut[:, odd, c * P:(c + 1) * P],
                                         w2s[:, bass.ds(e * (FC * D) + c * D, D)], start=(c == 0), stop=(c == FC - 1))
                    last.then_inc(p_y, 1)

            for k in range(-1, TILES + 2):
                step(k, odd=k % 2)


def kernel(x, ctx_1024, mask_BxSxS2_bk1, L0_xattn_W_merge, L0_xattn_b_merge, L0_ffn_router_w, L0_ffn_router_b,
           L0_ffn_w1, L0_ffn_w2):
    import concourse.bacc as bacc
    from concourse.bass_utils import run_bass_kernel_spmd

    a = np.ascontiguousarray
    ctx = np.asarray(ctx_1024)
    ins = {
        "x": a(np.asarray(x).transpose(1, 0, 2)),
        "ctx_k": a(ctx.transpose(1, 0, 2).reshape(K, B * D)),
        "ctx_t": a(ctx.transpose(2, 0, 1).reshape(D, B * K)),
        "ctx_one": np.ones((1, B * D), np.float32),
        "mask": a(np.asarray(mask_BxSxS2_bk1).transpose(1, 0, 2).reshape(S, B * K)),
        "w_t": a(np.asarray(L0_xattn_W_merge).T),
        "w_n": a(np.asarray(L0_xattn_W_merge)),
        "b_row": np.concatenate([np.asarray(L0_xattn_b_merge), np.zeros(E, np.float32)]).reshape(1, GW),
        "b_col": a(np.asarray(L0_xattn_b_merge).reshape(D, 1)),
        "router_w": a(np.asarray(L0_ffn_router_w)),
        "router_b": a(np.asarray(L0_ffn_router_b)),
        "w1": a(np.asarray(L0_ffn_w1).transpose(1, 0, 2).reshape(D, E * 2 * F)),
        "w2": a(np.asarray(L0_ffn_w2).reshape(E, FC, P, D).transpose(2, 0, 1, 3).reshape(P, E * FC * D)),
        "const": constants(),
    }
    nc = bacc.Bacc("TRN2", target_bir_lowering=False, num_devices=1)
    args = {n: nc.dram_tensor(f"in_{n}", v.shape, mybir.dt.from_np(v.dtype), kind="ExternalInput").ap() for n, v in ins.items()}
    out = nc.dram_tensor("out_rows", (TOKENS, D), F32, kind="ExternalOutput").ap()
    build(nc, out=out, **args)
    r = run_bass_kernel_spmd(nc, [{f"in_{n}": v for n, v in ins.items()}], core_ids=[0])
    return r.results[0]["out_rows"].reshape(S, B, D).transpose(1, 0, 2)
```

```python
from contextlib import ExitStack

import numpy as np
import concourse.bass as bass
from concourse import mybir

ALU = mybir.AluOpType
ACT = mybir.ActivationFunctionType
AX = mybir.AxisListType
F32 = mybir.dt.float32
F32R = mybir.dt.float32r
BF16 = mybir.dt.bfloat16
I32 = mybir.dt.int32
U32 = mybir.dt.uint32

P = 128
B, S, D = 32, 128, 128
K = 77
E, F = 8, 512
TOKENS = B * S
GB = 4
NG = B // GB
TILES = TOKENS // P + E - 1
AHEAD = 8
NQ = 4
TMIN = TOKENS // P
TPAD = TILES + TILES % 2
GW = D + E
SW = K + E
ROW = D + 4
MEAN, RSTD, PROB = D, D + 1, D + 2
FC = F // P
WCH = 512
NWP = E * 2 * F // WCH
WQ = NWP // 4
BSTEP = 8
SCALE = float(1.0 / np.sqrt(np.float32(D)))
NEG = -1.0e9
EPS = 1.0e-5
ROUND = 1.5 * 2.0 ** 23
EARLY = 8
FAR = 2 * TOKENS

C_ID, C_CEN, C_TRI, C_IOTA = 0, P, 2 * P, 3 * P
C_BAT = 4 * P
C_PB = C_BAT + B
C_KEEP = C_PB + 1
C_EM = C_KEEP + B * E
C_ONE = C_EM + E
C_ALL = C_ONE + E


def constants():
    c = np.zeros((P, C_ALL), np.float32)
    c[:, C_ID:C_ID + P] = np.eye(P)
    c[:, C_CEN:C_CEN + P] = np.eye(P) - 1.0 / P
    c[:, C_TRI:C_TRI + P] = np.triu(np.ones((P, P)), 1)
    c[:, C_IOTA:C_IOTA + P] = np.arange(P)
    c[:, C_BAT:C_BAT + B] = np.arange(B) + 1
    c[:, C_PB] = np.arange(P) * B
    c[:, C_KEEP:C_KEEP + B * E] = np.tile(np.arange(B) > 0, E)
    c[:, C_EM:C_EM + E] = np.arange(E) - E
    c[:, C_ONE:C_ONE + E] = 1.0
    return c


def build(nc, x, ctx_k, ctx_t, ctx_one, mask, w_t, w_n, b_row, b_col, router_w, router_b, w1, w2, const, out):
    x1_rows = nc.dram_tensor("x1_rows", (TOKENS, ROW), F32, kind="Internal").ap()

    with ExitStack() as keep:
        def sb(name, shape, dt=F32, stack=keep):
            return stack.enter_context(nc.sbuf_tensor(name, shape, dt))

        def sem(name):
            return keep.enter_context(nc.semaphore(name))

        cst = sb("cst", [P, C_ALL])
        w1hi = sb("w1hi", [P, E * 2 * F], F32R)
        w1lo = sb("w1lo", [P, E * 2 * F], F32R)
        w2s = sb("w2s", [P, E * FC * D])
        x1 = sb("x1", [P, B, ROW])
        onehot = sb("onehot", [P, E, B], BF16)
        tri = sb("tri", [P, P], BF16)
        ones = sb("ones", [P, P], BF16)
        numbers = sb("numbers", [P, P, B], BF16)
        batno = sb("batno", [P, B], BF16)
        gather_at = sb("gather_at", [P, TPAD], U32)
        scatter_at = sb("scatter_at", [P, TPAD], U32)
        silu_first = sb("silu_first", [P, 1])
        tiles_used = sb("tiles_used", [P, 1], I32)
        tile_expert = sb("tile_expert", [P, TPAD], I32)

        early = ExitStack()
        xs = sb("xs", [P, B, D], F32, early)
        ctxk = sb("ctxk", [K + 1, B * D], F32, early)
        ctxt = sb("ctxt", [P, B * K], F32, early)
        ctxc = sb("ctxc", [P, 2, GB, SW], F32, early)
        msk = sb("msk", [P, B * K], mybir.dt.uint8, early)
        wt = sb("wt", [P, GW], F32, early)
        wn = sb("wn", [P, D], F32, early)
        bcol = sb("bcol", [P, 1], F32, early)
        bcols = sb("bcols", [P, P], F32, early)
        brw = sb("brw", [P, E], F32, early)
        xrw = sb("xrw", [P, B, E], F32, early)
        rw = sb("rw", [P, E], F32, early)
        rwc = sb("rwc", [P, E], F32, early)
        rb = sb("rb", [P, E], F32, early)
        xt = sb("xt", [P, 2, GB * S], F32, early)
        prob = sb("prob", [P, 2, GB, K], F32, early)
        att = sb("att", [P, 2, GB, K], F32, early)
        merged = sb("merged", [K + 1, 2, GB * GW], F32, early)
        bn = sb("bn", [P, 2, GB, 6], F32, early)
        mv = sb("mv", [P, B, 2], F32, early)
        half = sb("half", [P, GB], F32, early)
        ve = sb("ve", [P, B], F32, early)
        rstd = sb("rstd", [P, B], F32, early)
        rs = sb("rs", [P, B], F32, early)
        fill = sb("fill", [P, B], F32, early)
        nmax = sb("nmax", [P, B], F32, early)
        nbias = sb("nbias", [P, B], F32, early)
        esum = sb("esum", [P, B], F32, early)
        einv = sb("einv", [P, B], F32, early)
        ve2 = sb("ve2", [P, B], F32, early)
        lg0 = sb("lg0", [P, B, E], F32, early)
        lg1 = sb("lg1", [P, B, E], F32, early)
        lg = sb("lg", [P, B, E], F32, early)
        lmax = sb("lmax", [P, B], F32, early)
        ldif = sb("ldif", [P, B, E], F32, early)
        lexp = sb("lexp", [P, B, E], F32, early)
        lsum = sb("lsum", [P, B], F32, early)
        cand = sb("cand", [P, B, E], F32, early)
        emin = sb("emin", [P, B], F32, early)
        wraw = sb("wraw", [P, 3 * WQ * WCH], F32, early)
        early.close()

        late = keep
        pre = sb("pre", [P, E, B])
        tl0 = sb("tl0", [P, E])
        tl = sb("tl", [P, E])
        tend = sb("tend", [P, E])
        tbeg = sb("tbeg", [P, E])
        sl0 = sb("sl0", [P, E, B])
        sl1 = sb("sl1", [P, E, B])
        sl2 = sb("sl2", [P, E, B])
        sl3 = sb("sl3", [P, E, B])
        slot = sb("slot", [P, B])
        jt0 = sb("jt0", [P, B])
        jt = sb("jt", [P, B], BF16)
        rm = sb("rm", [P, B], BF16)
        tcmp = sb("tcmp", [P, TPAD, E])
        tcnt = sb("tcnt", [P, TPAD])
        inv0 = sb("inv0", [P, TPAD])
        inv = sb("inv", [P, TPAD])
        vz = sb("vz", [P, TPAD])
        a0 = sb("a0", [P, TPAD, B], BF16)
        amat = sb("amat", [P, 2, TPAD, B], BF16)
        bmat = sb("bmat", [P, P, B], BF16)
        rows = sb("rows", [P, TILES, ROW])
        hg = sb("hg", [P, 2, D])
        hthi = sb("hthi", [P, 2, P], F32R)
        htlo = sb("htlo", [P, 2, P], F32R)
        sa = sb("sa", [P, 2, F])
        u = sb("u", [P, 2, F])
        ut = sb("ut", [P, 2, F])

        banks = keep.enter_context(nc.psum_tensor("banks", [P, 8 * 512], F32))
        bank = [banks[:, i * 512:(i + 1) * 512] for i in range(8)]
        ps_xt, ps_cc, ps_s = bank[0], bank[1], bank[2:4]
        ps_g, ps_o = (banks[:, i * 512:(i + 2) * 512].rearrange("p (h c) -> p h c", h=2)[:, :, 0:2 * GW] for i in (4, 6))
        ps_rank, ps_cnt, ps_inv = bank[0], bank[1], bank[2]
        ps_a, ps_g3, ps_ut, ps_ht, ps_y = bank[0:2], bank[2:4], bank[4:6], bank[6], bank[7]

        l_const, l_const2, l_rw, l_merge, l_rb, l_mask, l_ones, l_w2 = (
            sem(n) for n in ("l_const", "l_const2", "l_rw", "l_merge", "l_rb", "l_mask", "l_ones", "l_w2"))
        l_x = [sem(f"l_x{g}") for g in range(NG)]
        l_ctxk = [sem(f"l_ctxk{i}") for i in range(2)]
        l_ctxt = [sem(f"l_ctxt{i}") for i in range(2)]
        l_w1 = [sem(f"l_w1{i}") for i in range(4)]
        s_rows = sem("s_rows")
        p_xt, p_cc, p_s, p_g, p_o = (sem(n) for n in ("p_xt", "p_cc", "p_s", "p_g", "p_o"))
        p_rwc, p_router = sem("p_rwc"), sem("p_router")
        a_xt, a_cc, a_exp, a_g, a_rexp, a_whi, a_num = (sem(n) for n in ("a_xt", "a_cc", "a_exp", "a_g", "a_rexp", "a_whi", "a_num"))
        v_bf, v_rwc, v_router, v_bn, v_mv, v_rs, v_fill, v_mask, v_max, v_nb, v_xrw, v_inv = (
            sem(n) for n in ("v_bf", "v_rwc", "v_router", "v_bn", "v_mv", "v_rs", "v_fill", "v_mask", "v_max", "v_nb", "v_xrw", "v_inv"))
        v_x1, v_bn2, v_mv2, v_lg0, v_lg1, v_lg, v_lmax, v_ldif, v_cand, v_emin, v_hot, v_lsum, v_prob = (
            sem(n) for n in ("v_x1", "v_bn2", "v_mv2", "v_lg0", "v_lg1", "v_lg", "v_lmax", "v_ldif", "v_cand", "v_emin", "v_hot", "v_lsum", "v_prob"))
        g_half, g_bcols, g_ve, g_rstd, g_att, g_ve2, g_rstd2, g_wlo = (
            sem(n) for n in ("g_half", "g_bcols", "g_ve", "g_rstd", "g_att", "g_ve2", "g_rstd2", "g_wlo"))
        p_rank, p_inv = sem("p_rank"), sem("p_inv")
        v_chain = sem("v_chain")
        v_tl0, v_tl, v_sl0, v_sl1, v_tcnt = (sem(n) for n in ("v_tl0", "v_tl", "v_sl0", "v_sl1", "v_tcnt"))
        v_a0, v_am, a_am, v_bm, v_gat, v_sca, v_te = (sem(n) for n in ("v_a0", "v_am", "a_am", "v_bm", "v_gat", "v_sca", "v_te"))
        g_rows = [sem(f"g_rows{i}") for i in range(NQ)]
        g_out = sem("g_out")
        p_ht, p_a, p_gg, p_ut, p_y = (sem(n) for n in ("p_ht", "p_a", "p_gg", "p_ut", "p_y"))
        a_hthi, a_sa, a_ut = sem("a_hthi"), sem("a_sa"), sem("a_ut")
        v_hg, v_htlo, v_u, v_y = sem("v_hg"), sem("v_htlo"), sem("v_u"), sem("v_y")

        def group(t, g):
            return t[:, GB * g:GB * g + GB]

        def wpiece(i):
            r = i % (3 * WQ)
            return [wraw[:, r * WCH:(r + 1) * WCH]] + [w[:, i * WCH:(i + 1) * WCH] for w in (w1hi, w1lo)]

        def early(k):
            return max(0, min(EARLY, k - 1 + (k >= NG - 1)))

        def stage(g, part):
            if 0 <= g < NG:
                part(g)

        def load_tiles(eng):
            eng.wait_ge(v_te, 2)
            return eng.value_load(tiles_used[0:1, 0:1], min_val=TMIN, max_val=TILES)

        def last_steps(eng, step, ahead, used, t):
            if t == TILES:
                for k in range(t - ahead, t + 2):
                    step(k, t)
                return
            with eng.If(used > t):
                step(t - ahead, TILES)
                last_steps(eng, step, ahead, used, t + 1)
                eng.wait_ge(v_te, 2)
            with eng.Else():
                for k in range(t - ahead, t + 2):
                    step(k, t)

        block = keep.enter_context(nc.Block())

        @block.sync
        def _(sp):
            half, quarter = B // 2, NWP * WCH // 4

            def load_ctxt(h):
                cols = slice((0, 2 * GB * K)[h], (2 * GB * K, B * K)[h])
                sp.dma_start(ctxt[:, cols], ctx_t[:, cols]).then_inc(l_ctxt[h], 16)

            def load_ctxk(h):
                sp.dma_start(ctxk[0:K, h * half * D:(h + 1) * half * D], ctx_k[:, h * half * D:(h + 1) * half * D]).then_inc(l_ctxk[h], 16)

            def load_x(g):
                sp.dma_start(group(xs, g), x[:, GB * g:GB * g + GB, :]).then_inc(l_x[g], 16)

            def load_w1(q):
                sp.dma_start(wraw[:, q % 3 * quarter:(q % 3 + 1) * quarter], w1[:, q * quarter:(q + 1) * quarter]).then_inc(l_w1[q], 16)

            load_x(0)
            sp.dma_start(cst[:, 0:C_TRI], const[:, 0:C_TRI]).then_inc(l_const, 16)
            load_ctxt(0)
            sp.dma_start(rw[:], router_w).then_inc(l_rw, 16)
            sp.dma_start(msk[:], mask).then_inc(l_mask, 16)
            load_x(1)
            sp.dma_start(bcol[:], b_col).then_inc(l_merge, 16)
            sp.dma_start(wn[:], w_n).then_inc(l_merge, 16)
            sp.dma_start(wt[:, 0:D], w_t).then_inc(l_merge, 16)
            load_ctxk(0)
            sp.dma_start(ctxk[K:K + 1, :], ctx_one).then_inc(l_ones, 16)
            sp.dma_start(merged[K:K + 1, :, :].rearrange("k i (j d) -> k (i j) d", d=GW),
                         b_row.unsqueeze(1).to_broadcast([1, 2 * GB, GW])).then_inc(l_ones, 16)
            sp.dma_start(cst[:, C_TRI:C_ALL], const[:, C_TRI:C_ALL]).then_inc(l_const2, 16)
            load_x(2)
            sp.dma_start(rb[:], router_b.partition_broadcast(P)).then_inc(l_rb, 16)
            load_ctxt(1)
            load_x(3)
            load_w1(0)
            load_x(4)
            load_x(5)
            load_ctxk(1)
            load_x(6)
            load_x(7)
            load_w1(1)
            load_w1(2)
            sp.dma_start(w2s[:], w2).then_inc(l_w2, 16)
            sp.wait_ge(g_wlo, WQ)
            load_w1(3)
            for g in range(NG):
                sp.wait_ge(v_prob, g + 1)
                sp.wait_ge(g_rstd2, g + 1)
                sp.dma_start(x1_rows.rearrange("(l b) c -> l b c", b=B)[:, GB * g:GB * g + GB, :],
                             group(x1, g)).then_inc(s_rows, 16)

        @block.gpsimd
        def _(pool):
            nc.gpsimd.memset(half[:], -0.5).then_inc(g_half, 1)
            pool.wait_ge(g_half, 1)

            def w_lo(i):
                raw, hi, lo = wpiece(i)
                pool.wait_ge(a_whi, i + 1)
                pool.tensor_tensor(lo, raw, hi.bitcast(F32), ALU.subtract).then_inc(g_wlo, 1)

            def rstd1(g):
                pool.wait_ge(v_mv, g + 1)
                pool.tensor_scalar(group(ve, g), mv[:, GB * g:GB * g + GB, 1], EPS, None, ALU.add).then_inc(g_ve, 1)
                pool.wait_ge(g_ve, g + 1)
                pool.tensor_tensor(group(rstd, g), group(ve, g), half[:], ALU.pow).then_inc(g_rstd, 1)

            def rstd2(g):
                pool.wait_ge(v_mv2, g + 1)
                pool.tensor_scalar(group(ve2, g), x1[:, GB * g:GB * g + GB, RSTD], EPS, None, ALU.add).then_inc(g_ve2, 1)
                pool.wait_ge(g_ve2, g + 1)
                pool.tensor_tensor(x1[:, GB * g:GB * g + GB, RSTD], group(ve2, g), half[:], ALU.pow).then_inc(g_rstd2, 1)

            def weights(g):
                pool.wait_ge(v_inv, g + 1)
                if g >= 2:
                    pool.wait_ge(p_g, g - 1)
                pool.tensor_tensor(att[:, g % 2], prob[:, g % 2], group(einv, g).unsqueeze(2).to_broadcast([P, GB, K]),
                                   ALU.mult).then_inc(g_att, 1)

            pool.wait_ge(l_merge, 48)
            pool.tensor_copy(bcols[:], bcol[:].to_broadcast([P, P])).then_inc(g_bcols, 1)
            for k in range(-1, NG + 4):
                stage(k + 1, rstd1)
                stage(k - 1, weights)
                stage(k - 3, rstd2)
                for i in range(early(k - 1), early(k)):
                    w_lo(i)
            for i in range(EARLY, NWP):
                w_lo(i)

            def gather(i):
                if i == 0:
                    pool.wait_ge(v_gat, 1)
                    pool.wait_ge(s_rows, 16 * NG)
                if i >= NQ:
                    pool.wait_ge(g_rows[i % NQ], 16 * (i // NQ))
                pool.indirect_dma_start(rows[:, i, :], None, x1_rows,
                                        bass.IndirectOffsetOnAxis(gather_at[:, i:i + 1], 0)).then_inc(g_rows[i % NQ], 16)

            def scatter(i):
                if i == 0:
                    pool.wait_ge(v_sca, 1)
                pool.wait_ge(v_y, i + 1)
                pool.indirect_dma_start(out, bass.IndirectOffsetOnAxis(scatter_at[:, i:i + 1], 0), rows[:, i, 0:D], None,
                                        bounds_check=TOKENS - 1, oob_is_err=False).then_inc(g_out, 16)

            def tile(i, end):
                if i < end:
                    gather(i)
                if AHEAD <= i < end + AHEAD:
                    scatter(i - AHEAD)

            def last_tiles(t):
                if t == TILES:
                    for i in range(t, t + AHEAD):
                        tile(i, t)
                    pool.wait_ge(g_out, 16 * t)
                    return
                with pool.If(used > t):
                    tile(t, TILES)
                    last_tiles(t + 1)
                    pool.wait_ge(v_te, 2)
                with pool.Else():
                    for i in range(t, t + AHEAD):
                        tile(i, t)
                    pool.wait_ge(g_out, 16 * t)

            for i in range(TMIN):
                if i == AHEAD:
                    used = load_tiles(pool)
                tile(i, TILES)
            last_tiles(TMIN)

        @block.scalar
        def _(act):
            def w_hi(i):
                raw, hi, _ = wpiece(i)
                act.wait_ge(l_w1[i // WQ], 16)
                act.activation(hi, raw, ACT.Copy).then_inc(a_whi, 1)

            def copy_xt(g):
                act.wait_ge(p_xt, g + 1)
                if g >= 2:
                    act.wait_ge(p_s, g - 1)
                act.activation(xt[:, g % 2, :], ps_xt[:, :], ACT.Copy).then_inc(a_xt, 1)

            def copy_ctx(g):
                act.wait_ge(p_cc, g + 1)
                act.activation(ctxc[:, g % 2, :, 0:K], ps_cc[:, 0:GB * K].rearrange("p (b k) -> p b k", b=GB),
                               ACT.Copy).then_inc(a_cc, 1)

            def copy_merged(g):
                act.wait_ge(p_g, g + 1)
                if g >= 2:
                    act.wait_ge(p_o, g - 1)
                act.activation(merged[0:K, g % 2, :].rearrange("k (h c) -> k h c", h=2), ps_g[0:K], ACT.Copy).then_inc(a_g, 1)

            def exponentials(g):
                act.wait_ge(v_nb, g + 1)
                if g >= 2:
                    act.wait_ge(g_att, g - 1)
                for j in range(GB):
                    b = GB * g + j
                    act.activation(prob[:, g % 2, j, :], ps_s[g % 2][:, j * SW:j * SW + K], ACT.Exp,
                                   bias=nbias[:, b:b + 1], scale=rs[:, b:b + 1],
                                   accum_out=esum[:, b:b + 1]).then_inc(a_exp, 1)

            def router_exponentials(g):
                act.wait_ge(v_ldif, g + 1)
                act.activation(group(lexp, g), group(ldif, g), ACT.Exp).then_inc(a_rexp, 1)

            for k in range(-1, NG + 5):
                if k < NG:
                    stage(k - 4, router_exponentials)
                stage(k + 1, copy_xt)
                stage(k + 1, copy_ctx)
                stage(k - 2, copy_merged)
                if k >= NG:
                    stage(k - 4, router_exponentials)
                for i in range(early(k - 1), early(k)):
                    w_hi(i)
                if 1 <= k < 5:
                    if k == 1:
                        act.wait_ge(l_const2, 16)
                    r = (k - 1) * (P // 4)
                    act.activation(numbers[:, r:r + P // 4, :], cst[:, C_IOTA + r:C_IOTA + r + P // 4].unsqueeze(2).to_broadcast([P, P // 4, B]),
                                   ACT.Copy).then_inc(a_num, 1)
                stage(k, exponentials)

            for i in range(EARLY, NWP - 2):
                w_hi(i)
            act.wait_ge(v_a0, 1)
            act.activation(amat[:, 0, :, :], a0[:], ACT.Copy, scale=cst[:, C_PB:C_PB + 1]).then_inc(a_am, 1)
            for i in range(NWP - 2, NWP):
                w_hi(i)
            act.activation(silu_first[:], cst[:, C_ONE:C_ONE + 1], ACT.Silu)

            def step(k, end):
                odd = k % 2
                if 0 <= k + 1 < end:
                    q = (odd + 1) % 2
                    act.wait_ge(p_ht, k + 2)
                    if k + 1 >= 2:
                        act.wait_ge(p_gg, k)
                    act.activation(hthi[:, q, :], ps_ht[:, 0:P], ACT.Copy).then_inc(a_hthi, 1)
                if 0 <= k < end:
                    act.wait_ge(p_a, k + 1)
                    if k >= 2:
                        act.wait_ge(v_u, k - 1)
                    act.activation(sa[:, odd, :], ps_a[odd][:, :], ACT.Silu).then_inc(a_sa, 1)
                if 0 <= k - 1 < end:
                    q = (odd + 1) % 2
                    act.wait_ge(p_ut, k)
                    if k - 1 >= 2:
                        act.wait_ge(p_y, k - 2)
                    act.activation(ut[:, q, :], ps_ut[q][:, :], ACT.Copy).then_inc(a_ut, 1)

            for k in range(-1, TMIN - 1):
                if k == 6:
                    used = load_tiles(act)
                step(k, TILES)
            last_steps(act, step, 1, used, TMIN)

        @block.vector
        def _(dve):
            def stats1(g):
                dve.wait_ge(l_x[g], 16)
                if g >= 1:
                    dve.wait_ge(v_mv, g)
                for j in range(GB):
                    dve.bn_stats(bn[:, 0, j, :], xs[:, GB * g + j, :]).then_inc(v_bn, 1)

            def mean1(g):
                dve.wait_ge(v_bn, GB * (g + 1))
                for j in range(GB):
                    last = dve.bn_aggr(mv[:, GB * g + j, :], bn[:, 0, j, :])
                last.then_inc(v_mv, 1)

            def scales(g):
                dve.wait_ge(g_rstd, g + 1)
                dve.tensor_scalar(group(rs, g), group(rstd, g), SCALE, None, ALU.mult).then_inc(v_rs, 1)
                dve.scalar_tensor_tensor(group(fill, g), group(ve, g), NEG / SCALE, group(rstd, g), ALU.mult, ALU.mult).then_inc(v_fill, 1)

            def batches(t, g):
                return t[g % 2][:, 0:GB * SW].rearrange("p (b k) -> p b k", b=GB)

            def x_router(g):
                dve.wait_ge(p_s, g + 1)
                dve.tensor_tensor(group(xrw, g), batches(ps_s, g)[:, :, K:SW], brw[:].unsqueeze(1).to_broadcast([P, GB, E]),
                                  ALU.add).then_inc(v_xrw, 1)

            def fill_masked(g):
                dve.wait_ge(v_fill, g + 1)
                if g == 0:
                    dve.wait_ge(l_mask, 16)
                dve.copy_predicated(batches(ps_s, g)[:, :, 0:K], msk[:, g * GB * K:(g + 1) * GB * K].rearrange("p (b k) -> p b k", b=GB),
                                    group(fill, g).unsqueeze(2).to_broadcast([P, GB, K])).then_inc(v_mask, 1)

            def maximum(g):
                dve.wait_ge(v_mask, g + 1)
                dve.tensor_reduce(group(nmax, g), batches(ps_s, g)[:, :, 0:K], AX.X, ALU.max, negate=True).then_inc(v_max, 1)

            def exp_bias(g):
                dve.wait_ge(v_max, g + 1)
                dve.wait_ge(v_rs, g + 1)
                dve.tensor_tensor(group(nbias, g), group(nmax, g), group(rs, g), ALU.mult).then_inc(v_nb, 1)

            def inverse_sum(g):
                dve.wait_ge(a_exp, GB * (g + 1))
                dve.reciprocal(group(einv, g), group(esum, g)).then_inc(v_inv, 1)

            halves = ps_o.rearrange("p h (b c) -> p h b c", b=2)

            def residual(g):
                dve.wait_ge(p_o, g + 1)
                dve.tensor_tensor(x1[:, GB * g:GB * g + GB, 0:D].rearrange("p (h b) d -> p h b d", h=2), halves[:, :, :, 0:D],
                                  group(xs, g).rearrange("p (h b) d -> p h b d", h=2), ALU.add).then_inc(v_x1, 1)

            def stats2(g):
                dve.wait_ge(v_x1, g + 1)
                if g >= 1:
                    dve.wait_ge(v_mv2, g)
                for j in range(GB):
                    dve.bn_stats(bn[:, 1, j, :], x1[:, GB * g + j, 0:D]).then_inc(v_bn2, 1)

            def mean2(g):
                dve.wait_ge(v_bn2, GB * (g + 1))
                for j in range(GB):
                    last = dve.bn_aggr(x1[:, GB * g + j, MEAN:RSTD + 1], bn[:, 1, j, :])
                last.then_inc(v_mv2, 1)

            wide = [P, GB, E]

            def logits0(g):
                dve.wait_ge(p_o, g + 1)
                dve.wait_ge(v_xrw, g + 1)
                dve.tensor_tensor(group(lg0, g).rearrange("p (h b) e -> p h b e", h=2), halves[:, :, :, D:GW],
                                  group(xrw, g).rearrange("p (h b) e -> p h b e", h=2), ALU.add).then_inc(v_lg0, 1)

            def logits1(g):
                dve.wait_ge(v_lg0, g + 1)
                dve.wait_ge(g_rstd2, g + 1)
                dve.tensor_tensor(group(lg1, g), group(lg0, g), x1[:, GB * g:GB * g + GB, RSTD].unsqueeze(2).to_broadcast(wide),
                                  ALU.mult).then_inc(v_lg1, 1)

            def logits2(g):
                dve.wait_ge(v_lg1, g + 1)
                if g == 0:
                    dve.wait_ge(l_rb, 16)
                dve.tensor_tensor(group(lg, g), group(lg1, g), rb[:].unsqueeze(1).to_broadcast(wide), ALU.add).then_inc(v_lg, 1)

            def greatest(g):
                dve.wait_ge(v_lg, g + 1)
                dve.tensor_reduce(group(lmax, g), group(lg, g), AX.X, ALU.max).then_inc(v_lmax, 1)

            def differences(g):
                dve.wait_ge(v_lmax, g + 1)
                dve.tensor_tensor(group(ldif, g), group(lg, g), group(lmax, g).unsqueeze(2).to_broadcast(wide), ALU.subtract).then_inc(v_ldif, 1)

            def candidates(g):
                dve.wait_ge(v_ldif, g + 1)
                dve.scalar_tensor_tensor(group(cand, g), group(ldif, g), 0.0,
                                         cst[:, C_EM:C_EM + E].unsqueeze(1).to_broadcast(wide), ALU.is_ge, ALU.mult).then_inc(v_cand, 1)

            def first(g):
                dve.wait_ge(v_cand, g + 1)
                dve.tensor_reduce(group(emin, g), group(cand, g), AX.X, ALU.min).then_inc(v_emin, 1)

            def choice(g):
                dve.wait_ge(v_emin, g + 1)
                dve.tensor_tensor(onehot[:, :, GB * g:GB * g + GB].rearrange("p e b -> p b e"), cst[:, C_EM:C_EM + E].unsqueeze(1).to_broadcast(wide),
                                  group(emin, g).unsqueeze(2).to_broadcast(wide), ALU.is_equal).then_inc(v_hot, 1)

            def router_sum(g):
                dve.wait_ge(a_rexp, g + 1)
                dve.tensor_reduce(group(lsum, g), group(lexp, g), AX.X, ALU.add).then_inc(v_lsum, 1)

            def probability(g):
                dve.wait_ge(v_lsum, g + 1)
                dve.reciprocal(x1[:, GB * g:GB * g + GB, PROB], group(lsum, g)).then_inc(v_prob, 1)

            def router(g, begun=False):
                if not begun:
                    logits1(g)
                    logits2(g)
                greatest(g)
                differences(g)
                candidates(g)
                first(g)
                choice(g)
                router_sum(g)
                probability(g)

            dve.memset(x1[:, :, PROB + 1:ROW], 0.0).then_inc(v_bf, 1)
            dve.memset(ones[:], 1.0).then_inc(v_bf, 1)
            stats1(0)
            dve.wait_ge(p_rwc, 1)
            dve.tensor_copy(rwc[:], ps_g[:, 0, 0:E]).then_inc(v_rwc, 1)
            dve.tensor_copy(ctxc[:, :, :, K:SW].rearrange("p i b e -> p (i b) e"),
                            ps_g[:, 0, 0:E].unsqueeze(1).to_broadcast([P, 2 * GB, E])).then_inc(v_rwc, 1)
            mean1(0)
            stats1(1)
            dve.wait_ge(p_router, 1)
            dve.tensor_copy(wt[:, D:GW], ps_g[:, 1, 0:E]).then_inc(v_router, 1)
            dve.tensor_copy(brw[:], ps_g[:, 1, E:2 * E]).then_inc(v_router, 1)
            mean1(1)
            for k in range(NG):
                if k == 1:
                    dve.wait_ge(l_const2, 16)
                    dve.tensor_copy(tri[:], cst[:, C_TRI:C_TRI + P]).then_inc(v_bf, 1)
                    dve.tensor_copy(batno[:], cst[:, C_BAT:C_BAT + B]).then_inc(v_bf, 1)
                stage(k - 4, greatest)
                stage(k - 1, inverse_sum)
                stage(k - 4, differences)
                stage(k - 3, stats2)
                stage(k - 4, candidates)
                stage(k - 3, mean2)
                stage(k - 4, first)
                stage(k, scales)
                if k == 0:
                    dve.wait_ge(v_router, 2)
                stage(k, x_router)
                stage(k - 4, choice)
                stage(k, fill_masked)
                stage(k - 4, router_sum)
                stage(k, maximum)
                stage(k - 2, logits0)
                stage(k, exp_bias)
                stage(k - 2, residual)
                stage(k - 4, probability)
                stage(k + 2, stats1)
                stage(k - 3, logits1)
                stage(k + 2, mean1)
                stage(k - 3, logits2)

            inverse_sum(NG - 1)
            for g in range(NG - 4, NG):
                if g >= NG - 2:
                    logits0(g)
                    residual(g)
                if g >= NG - 3:
                    stats2(g)
                    mean2(g)
                if g >= NG - 2:
                    router(g - 1)
                if g == NG - 4:
                    router(g, begun=True)
            router(NG - 1)

            steps = [0]

            def then(ins):
                steps[0] += 1
                ins.then_inc(v_chain, 1)
                dve.wait_ge(v_chain, steps[0])

            dve.wait_ge(p_rank, 1)
            cnt3 = ps_cnt[:, 0:E * B].rearrange("p (e b) -> p e b", e=E)
            rank3 = ps_rank[:, 0:E * B].rearrange("p (e b) -> p e b", e=E)
            wide = [P, E, B]
            then(dve.tensor_tensor_scan(pre[:].rearrange("p e b -> p (e b)"), cst[:, C_KEEP:C_KEEP + E * B],
                                        ps_cnt[:, 0:E * B], 0.0, ALU.mult, ALU.add))
            dve.tensor_scalar(tl0[:], pre[:, :, B - 1], P / 2 - 0.5, 1.0 / P, ALU.add, ALU.mult).then_inc(v_tl0, 1)
            dve.tensor_tensor(sl0[:], pre[:], cnt3, ALU.subtract).then_inc(v_sl0, 1)
            dve.wait_ge(v_tl0, 1)
            dve.tensor_scalar(tl[:], tl0[:], ROUND, ROUND, ALU.add, ALU.subtract).then_inc(v_tl, 1)
            dve.wait_ge(v_sl0, 1)
            dve.tensor_tensor(sl1[:], sl0[:], rank3, ALU.add).then_inc(v_sl1, 1)
            dve.wait_ge(v_tl, 1)
            then(dve.tensor_tensor_scan(tend[:], cst[:, C_ONE:C_ONE + E], tl[:], 0.0, ALU.mult, ALU.add))
            then(dve.tensor_tensor(tbeg[:], tend[:], tl[:], ALU.subtract))
            dve.wait_ge(v_sl1, 1)
            then(dve.scalar_tensor_tensor(sl2[:], tbeg[:].unsqueeze(2).to_broadcast(wide), float(P), sl1[:], ALU.mult, ALU.add))
            then(dve.tensor_tensor(sl3[:], sl2[:], onehot[:], ALU.mult))
            then(dve.tensor_reduce(slot[:], sl3[:].rearrange("p e b -> p b e"), AX.X, ALU.add))
            then(dve.tensor_scalar(jt0[:], slot[:], -(P / 2 - 0.5), 1.0 / P, ALU.add, ALU.mult))
            then(dve.tensor_scalar(jt[:], jt0[:], ROUND, ROUND, ALU.add, ALU.subtract))
            wide = [P, TPAD, B]
            dve.wait_ge(a_num, 4)
            dve.tensor_tensor(a0[:], numbers[:, 0:TPAD, :], jt[:].unsqueeze(1).to_broadcast(wide), ALU.is_equal).then_inc(v_a0, 1)
            then(dve.scalar_tensor_tensor(rm[:], jt[:], -float(P), slot[:], ALU.mult, ALU.add))
            for b in range(0, B, BSTEP):
                if b == BSTEP:
                    dve.wait_ge(v_a0, 1)
                    dve.tensor_tensor(amat[:, 1, :, :], a0[:], batno[:].unsqueeze(1).to_broadcast(wide), ALU.mult).then_inc(v_am, 1)
                dve.tensor_tensor(bmat[:, :, b:b + BSTEP], numbers[:, :, b:b + BSTEP],
                                  rm[:, b:b + BSTEP].unsqueeze(1).to_broadcast([P, P, BSTEP]), ALU.is_equal).then_inc(v_bm, 1)
            wide = [P, TPAD, E]
            then(dve.tensor_tensor(tcmp[:], tend[:].unsqueeze(1).to_broadcast(wide),
                                   cst[:, C_IOTA:C_IOTA + TPAD].unsqueeze(2).to_broadcast(wide), ALU.is_le))
            dve.tensor_reduce(tcnt[:], tcmp[:], AX.X, ALU.add).then_inc(v_tcnt, 1)
            dve.wait_ge(p_inv, 1)
            then(dve.tensor_copy(inv0[:], ps_inv[:, 0:TPAD]))
            then(dve.tensor_tensor(inv[:], ps_inv[:, TPAD:2 * TPAD], inv0[:], ALU.add))
            dve.tensor_scalar(gather_at[:], inv[:], 1.0, 1.0, ALU.max, ALU.subtract).then_inc(v_gat, 1)
            dve.wait_ge(v_tcnt, 1)
            dve.tensor_scalar(tile_expert[:], tcnt[:], float(E - 1), None, ALU.min).then_inc(v_te, 1)
            dve.tensor_copy(tiles_used[:], tend[:, E - 1:E]).then_inc(v_te, 1)
            then(dve.tensor_scalar(vz[:], inv[:], 0.0, float(FAR + 1), ALU.is_equal, ALU.mult))
            dve.scalar_tensor_tensor(scatter_at[:], inv[:], -1.0, vz[:], ALU.add, ALU.add).then_inc(v_sca, 1)

            def low_part(t):
                dve.wait_ge(a_hthi, t + 1)
                if t >= 2:
                    dve.wait_ge(p_gg, t - 1)
                dve.tensor_tensor(htlo[:, t % 2, :], ps_ht[:, 0:P], hthi[:, t % 2, :].bitcast(F32), ALU.subtract).then_inc(v_htlo, 1)

            def step(k, end):
                odd = k % 2
                if k == -1:
                    low_part(0)
                if 0 <= k + 2 < end:
                    dve.wait_ge(g_rows[(k + 2) % NQ], 16 * ((k + 2) // NQ + 1))
                    if k + 2 >= 2:
                        dve.wait_ge(p_ht, k + 1)
                    row = rows[:, k + 2, :]
                    dve.tensor_scalar(hg[:, odd, :], row[:, 0:D], row[:, MEAN:MEAN + 1], row[:, RSTD:RSTD + 1],
                                      ALU.subtract, ALU.mult).then_inc(v_hg, 1)
                if 1 <= k + 1 < end:
                    low_part(k + 1)
                if 0 <= k < end:
                    dve.wait_ge(p_gg, k + 1)
                    dve.wait_ge(a_sa, k + 1)
                    if k >= 2:
                        dve.wait_ge(p_ut, k - 1)
                    dve.tensor_tensor(u[:, odd, :], ps_g3[odd][:, :], sa[:, odd, :], ALU.mult).then_inc(v_u, 1)
                if 0 <= k - 2 < end:
                    dve.wait_ge(p_y, k - 1)
                    row = rows[:, k - 2, :]
                    dve.scalar_tensor_tensor(row[:, 0:D], ps_y[:, 0:D], row[:, PROB:PROB + 1], row[:, 0:D],
                                             ALU.mult, ALU.add).then_inc(v_y, 1)

            for k in range(-2, TMIN - 2):
                if k == 6:
                    used = load_tiles(dve)
                step(k, TILES)
            last_steps(dve, step, 2, used, TMIN)

        @block.tensor
        def _(pe):
            ident = cst[:, C_ID:C_ID + P]
            centre = cst[:, C_CEN:C_CEN + P]

            def turn_x(g):
                if g == 0:
                    pe.wait_ge(l_const, 16)
                pe.wait_ge(l_x[g], 16)
                if g >= 1:
                    pe.wait_ge(a_xt, g)
                for j in range(GB):
                    last = pe.transpose(ps_xt[:, j * S:(j + 1) * S], xs[:, GB * g + j, :], ident)
                last.then_inc(p_xt, 1)

            def centre_ctx(g):
                pe.wait_ge(l_ctxt[0 if g < 2 else 1], 16)
                if g >= 1:
                    pe.wait_ge(a_cc, g)
                pe.matmul(ps_cc[:, 0:GB * K], centre, ctxt[:, g * GB * K:(g + 1) * GB * K], start=True, stop=True).then_inc(p_cc, 1)

            def scores(g):
                pe.wait_ge(a_xt, g + 1)
                pe.wait_ge(a_cc, g + 1)
                if g == 0:
                    pe.wait_ge(v_rwc, 2)
                if g >= 2:
                    pe.wait_ge(a_exp, GB * (g - 1))
                for j in range(GB):
                    last = pe.matmul(ps_s[g % 2][:, j * SW:(j + 1) * SW], xt[:, g % 2, j * S:(j + 1) * S],
                                     ctxc[:, g % 2, j, :], start=True, stop=True)
                last.then_inc(p_s, 1)

            def merge(g):
                pe.wait_ge(g_att, g + 1)
                if g == 0:
                    pe.wait_ge(v_router, 2)
                if g >= 1:
                    pe.wait_ge(a_g, g)
                for j in range(GB):
                    last = pe.matmul(ps_g[0:K, j // 2, j % 2 * GW:(j % 2 + 1) * GW], att[:, g % 2, j, :], wt[:], start=True, stop=True)
                last.then_inc(p_g, 1)

            def output(g):
                pe.wait_ge(a_g, g + 1)
                pe.wait_ge(l_ctxk[g * 2 // NG], 16)
                if g == 0:
                    pe.wait_ge(l_ones, 32)
                if g >= 1:
                    pe.wait_ge(v_x1, g)
                    pe.wait_ge(v_lg0, g)
                for j in range(GB):
                    last = pe.matmul(ps_o[:, j // 2, j % 2 * GW:(j % 2 + 1) * GW], ctxk[:, (GB * g + j) * D:(GB * g + j + 1) * D],
                                     merged[:, g % 2, j * GW:(j + 1) * GW], start=True, stop=True)
                last.then_inc(p_o, 1)

            turn_x(0)
            pe.wait_ge(l_rw, 16)
            pe.matmul(ps_g[:, 0, 0:E], centre, rw[:], start=True, stop=True).then_inc(p_rwc, 1)
            centre_ctx(0)
            pe.wait_ge(v_rwc, 1)
            pe.wait_ge(l_merge, 48)
            pe.matmul(ps_g[:, 1, 0:E], wn[:], rwc[:], start=True, stop=True)
            pe.wait_ge(g_bcols, 1)
            pe.matmul(ps_g[:, 1, E:2 * E], bcols[:], rwc[:], start=True, stop=True).then_inc(p_router, 1)
            scores(0)
            for k in range(NG + 3):
                stage(k + 1, turn_x)
                stage(k + 1, centre_ctx)
                if k > 0:
                    stage(k, scores)
                if k < NG:
                    stage(k - 2, output)
                stage(k - 1, merge)
                if k >= NG:
                    stage(k - 2, output)

            pe.wait_ge(v_bf, 4)
            pe.wait_ge(v_hot, NG)
            pe.matmul(ps_rank[:, 0:E * B], tri[:], onehot[:].rearrange("p e b -> p (e b)"), start=True, stop=True)
            pe.matmul(ps_cnt[:, 0:E * B], ones[:], onehot[:].rearrange("p e b -> p (e b)"), start=True, stop=True).then_inc(p_rank, 1)
            pe.wait_ge(v_am, 1)
            pe.wait_ge(a_am, 1)
            for b in range(B):
                pe.wait_ge(v_bm, b // BSTEP + 1)
                last = pe.matmul(ps_inv[:, 0:2 * TPAD], bmat[:, :, b], amat[:, :, :, b], start=(b == 0), stop=(b == B - 1))
            last.then_inc(p_inv, 1)
            pe.wait_ge(v_te, 1)
            pe.wait_ge(a_whi, NWP)
            pe.wait_ge(g_wlo, NWP)
            pe.wait_ge(l_w2, 16)
            pe.wait_ge(v_sca, 1)

            def turn_input(t):
                pe.wait_ge(v_hg, t + 1)
                if t >= 1:
                    pe.wait_ge(v_htlo, t)
                pe.transpose(ps_ht[:, 0:P], hg[:, t % 2, :], ident).then_inc(p_ht, 1)

            experts = {}

            def step(k, end):
                odd = k % 2
                q = (odd + 1) % 2
                if 0 <= k + 1 < end and k != 0:
                    turn_input(k + 1)
                if 0 <= k < end:
                    e = experts[k] = pe.value_load(tile_expert[0:1, k:k + 1], min_val=0, max_val=E - 1)
                    pe.wait_ge(a_hthi, k + 1)
                    if k >= 2:
                        pe.wait_ge(v_u, k - 1)
                    for c, ps, done in ((0, ps_a[odd], p_a), (1, ps_g3[odd], p_gg)):
                        whi = w1hi[:, bass.ds(e * (2 * F) + c * F, F)]
                        wlo = w1lo[:, bass.ds(e * (2 * F) + c * F, F)]
                        pe.matmul(ps[:, :], hthi[:, odd, :], whi, start=True, stop=False)
                        pe.matmul(ps[:, :], hthi[:, odd, :], wlo, start=False, stop=False)
                        if c == 0:
                            pe.wait_ge(v_htlo, k + 1)
                        pe.matmul(ps[:, :], htlo[:, odd, :], whi, start=False, stop=True).then_inc(done, 1)
                        if k == 0 and c == 0:
                            turn_input(1)
                if 0 <= k - 1 < end:
                    pe.wait_ge(v_u, k)
                    if k - 1 >= 2:
                        pe.wait_ge(a_ut, k - 2)
                    for c in range(FC):
                        last = pe.transpose(ps_ut[q][:, c * P:(c + 1) * P], u[:, q, c * P:(c + 1) * P], ident)
                    last.then_inc(p_ut, 1)
                if 0 <= k - 2 < end:
                    pe.wait_ge(a_ut, k - 1)
                    if k - 2 >= 1:
                        pe.wait_ge(v_y, k - 2)
                    e = experts[k - 2]
                    for c in range(FC):
                        last = pe.matmul(ps_y[:, 0:D], ut[:, odd, c * P:(c + 1) * P],
                                         w2s[:, bass.ds(e * (FC * D) + c * D, D)], start=(c == 0), stop=(c == FC - 1))
                    last.then_inc(p_y, 1)

            for k in range(-1, TMIN - 1):
                if k == 6:
                    used = load_tiles(pe)
                step(k, TILES)
            last_steps(pe, step, 1, used, TMIN)


def kernel(x, ctx_1024, mask_BxSxS2_bk1, L0_xattn_W_merge, L0_xattn_b_merge, L0_ffn_router_w, L0_ffn_router_b,
           L0_ffn_w1, L0_ffn_w2):
    import concourse.bacc as bacc
    from concourse.bass_utils import run_bass_kernel_spmd

    a = np.ascontiguousarray
    ctx = np.asarray(ctx_1024)
    ins = {
        "x": a(np.asarray(x).transpose(1, 0, 2)),
        "ctx_k": a(ctx.transpose(1, 0, 2).reshape(K, B * D)),
        "ctx_t": a(ctx.transpose(2, 0, 1).reshape(D, B * K)),
        "ctx_one": np.ones((1, B * D), np.float32),
        "mask": a(np.asarray(mask_BxSxS2_bk1).transpose(1, 0, 2).reshape(S, B * K)),
        "w_t": a(np.asarray(L0_xattn_W_merge).T),
        "w_n": a(np.asarray(L0_xattn_W_merge)),
        "b_row": np.concatenate([np.asarray(L0_xattn_b_merge), np.zeros(E, np.float32)]).reshape(1, GW),
        "b_col": a(np.asarray(L0_xattn_b_merge).reshape(D, 1)),
        "router_w": a(np.asarray(L0_ffn_router_w)),
        "router_b": a(np.asarray(L0_ffn_router_b)),
        "w1": a(np.asarray(L0_ffn_w1).transpose(1, 0, 2).reshape(D, E * 2 * F)),
        "w2": a(np.asarray(L0_ffn_w2).reshape(E, FC, P, D).transpose(2, 0, 1, 3).reshape(P, E * FC * D)),
        "const": constants(),
    }
    nc = bacc.Bacc("TRN2", target_bir_lowering=False, num_devices=1)
    args = {n: nc.dram_tensor(f"in_{n}", v.shape, mybir.dt.from_np(v.dtype), kind="ExternalInput").ap() for n, v in ins.items()}
    out = nc.dram_tensor("out_rows", (TOKENS, D), F32, kind="ExternalOutput").ap()
    build(nc, out=out, **args)
    r = run_bass_kernel_spmd(nc, [{f"in_{n}": v for n, v in ins.items()}], core_ids=[0])
    return r.results[0]["out_rows"].reshape(S, B, D).transpose(1, 0, 2)
```
